# Optimizing a Trainium2 kernel written in Bass

```python
import numpy as np
import jax
import jax.numpy as jnp

def _softmax(x, axis=-1):
    return jax.nn.softmax(x, axis=axis)

def _gelu(x):
    return jax.nn.gelu(x, approximate=True)

def _silu(x):
    return jax.nn.silu(x)

def _sigmoid(x):
    return jax.nn.sigmoid(x)

def _layernorm(x, axis=-1, eps=1e-05):
    m = jnp.mean(x, axis=axis, keepdims=True)
    v = jnp.var(x, axis=axis, keepdims=True)
    return (x - m) / jnp.sqrt(v + eps)

def _scatter_add(tgt, idx, src, axis=0):
    return tgt.at[idx].add(src)

def _segment_sum(src, seg, n):
    return jax.ops.segment_sum(src, seg, n)
kernel_name = 'mk_adj_preln_d2_adj_r2_f9196b'

def setup_inputs(seed: int=0):
    np.random.seed(seed)
    _w = jnp.asarray

    def _rec_inputs():
        import jax
        import jax.numpy as jnp
        _gk = jax.random.key(seed)
        x = 7.22e-05 + 1 * jax.random.normal(jax.random.fold_in(_gk, 1), (64, 128, 128), jnp.float32)
        _a = jax.random.bernoulli(jax.random.fold_in(_gk, 2), 0.03125, (64, 128, 128))
        _a = jnp.logical_or(_a, jnp.swapaxes(_a, -1, -2))
        _a = jnp.logical_or(_a, jnp.eye(128, dtype=bool))
        _af = _a.astype(jnp.float32)
        adj = _af
        return (x, adj)
    x, adj = _rec_inputs()

    def _L0_gnn_setup():
        import jax, jax.numpy as jnp
        import numpy as np
        from jax import lax
        DIM = 128
        EPS = 1e-05

        def _bn(h, g, b, m, v):
            scale = g / jnp.sqrt(v + EPS)
            return h * scale[None, :, None] + (b - m * scale)[None, :, None]

        def _conv1d(h, w, pad):
            return lax.conv_general_dilated(h, w, window_strides=(1,), padding=[(pad, pad)], dimension_numbers=('NCH', 'OIH', 'NCH'))
        key = jax.random.key(seed)
        ks = jax.random.split(key, 16)
        bs, n, d = (16, 1024, DIM)
        s = 0.05
        return {'x': jax.random.normal(ks[0], (bs, n, d), jnp.float32), 'mask': jnp.ones((bs, n, n), jnp.float32), 'w_se': jax.random.normal(ks[1], (3, d), jnp.float32) * s, 'b_se': jnp.zeros((3,), jnp.float32), 'conv1_w': jax.random.normal(ks[2], (d, d, 1), jnp.float32) * s, 'bn1_g': jnp.ones((d,), jnp.float32), 'bn1_b': jnp.zeros((d,), jnp.float32), 'bn1_m': jnp.zeros((d,), jnp.float32), 'bn1_v': jnp.ones((d,), jnp.float32), 'conv2_w': jax.random.normal(ks[3], (d, d, 17), jnp.float32) * s, 'bn2_g': jnp.ones((d,), jnp.float32), 'bn2_b': jnp.zeros((d,), jnp.float32), 'bn2_m': jnp.zeros((d,), jnp.float32), 'bn2_v': jnp.ones((d,), jnp.float32), 'w_msg': jax.random.normal(ks[4], (d, d), jnp.float32) * s, 'b_msg': jnp.zeros((d,), jnp.float32), 'w_ih': jax.random.normal(ks[5], (3 * d, 2 * d), jnp.float32) * s, 'b_ih': jnp.zeros((3 * d,), jnp.float32), 'w_hh': jax.random.normal(ks[6], (3 * d, d), jnp.float32) * s, 'b_hh': jnp.zeros((3 * d,), jnp.float32)}
    _L0_gnn_all = _L0_gnn_setup()
    _L0_gnn_in = {k: v for k, v in _L0_gnn_all.items() if k in ('w_se', 'b_se', 'conv1_w', 'bn1_g', 'bn1_b', 'bn1_m', 'bn1_v', 'conv2_w', 'bn2_g', 'bn2_b', 'bn2_m', 'bn2_v', 'w_msg', 'b_msg', 'w_ih', 'b_ih', 'w_hh', 'b_hh')}
    del _L0_gnn_all

    def _L1_gnn_setup():
        import jax, jax.numpy as jnp
        import numpy as np
        key = jax.random.key(seed)
        k1, k2, k3, k4 = jax.random.split(key, 4)
        B, N, F_in, F_out = (8, 1024, 128, 128)
        x = jax.random.normal(k1, (B, N, F_in), dtype=jnp.float32)
        adj = jax.random.uniform(k2, (B, N, N), dtype=jnp.float32)
        stdv = 1.0 / np.sqrt(F_out)
        weight = jax.random.uniform(k3, (F_in, F_out), dtype=jnp.float32, minval=-stdv, maxval=stdv)
        bias = jax.random.uniform(k4, (F_out,), dtype=jnp.float32, minval=-stdv, maxval=stdv)
        return {'x': x, 'adj': adj, 'weight': weight, 'bias': bias}
    _L1_gnn_all = _L1_gnn_setup()
    _L1_gnn_in = {k: v for k, v in _L1_gnn_all.items() if k in ('weight', 'bias')}
    del _L1_gnn_all
    return {'x': x, 'adj': adj, 'L0_gnn_w_se': _L0_gnn_in['w_se'], 'L0_gnn_b_se': _L0_gnn_in['b_se'], 'L0_gnn_conv1_w': _L0_gnn_in['conv1_w'], 'L0_gnn_bn1_g': _L0_gnn_in['bn1_g'], 'L0_gnn_bn1_b': _L0_gnn_in['bn1_b'], 'L0_gnn_bn1_m': _L0_gnn_in['bn1_m'], 'L0_gnn_bn1_v': _L0_gnn_in['bn1_v'], 'L0_gnn_conv2_w': _L0_gnn_in['conv2_w'], 'L0_gnn_bn2_g': _L0_gnn_in['bn2_g'], 'L0_gnn_bn2_b': _L0_gnn_in['bn2_b'], 'L0_gnn_bn2_m': _L0_gnn_in['bn2_m'], 'L0_gnn_bn2_v': _L0_gnn_in['bn2_v'], 'L0_gnn_w_msg': _L0_gnn_in['w_msg'], 'L0_gnn_b_msg': _L0_gnn_in['b_msg'], 'L0_gnn_w_ih': _L0_gnn_in['w_ih'], 'L0_gnn_b_ih': _L0_gnn_in['b_ih'], 'L0_gnn_w_hh': _L0_gnn_in['w_hh'], 'L0_gnn_b_hh': _L0_gnn_in['b_hh'], 'L1_gnn_weight': _L1_gnn_in['weight'], 'L1_gnn_bias': _L1_gnn_in['bias']}

def reference(x, adj, L0_gnn_w_se, L0_gnn_b_se, L0_gnn_conv1_w, L0_gnn_bn1_g, L0_gnn_bn1_b, L0_gnn_bn1_m, L0_gnn_bn1_v, L0_gnn_conv2_w, L0_gnn_bn2_g, L0_gnn_bn2_b, L0_gnn_bn2_m, L0_gnn_bn2_v, L0_gnn_w_msg, L0_gnn_b_msg, L0_gnn_w_ih, L0_gnn_b_ih, L0_gnn_w_hh, L0_gnn_b_hh, L1_gnn_weight, L1_gnn_bias):
    import jax
    import jax.numpy as jnp

    def _L0_gnn_ref(x, mask, w_se, b_se, conv1_w, bn1_g, bn1_b, bn1_m, bn1_v, conv2_w, bn2_g, bn2_b, bn2_m, bn2_v, w_msg, b_msg, w_ih, b_ih, w_hh, b_hh):
        import jax, jax.numpy as jnp
        import numpy as np
        from jax import lax
        DIM = 128
        EPS = 1e-05

        def _bn(h, g, b, m, v):
            scale = g / jnp.sqrt(v + EPS)
            return h * scale[None, :, None] + (b - m * scale)[None, :, None]

        def _conv1d(h, w, pad):
            return lax.conv_general_dilated(h, w, window_strides=(1,), padding=[(pad, pad)], dimension_numbers=('NCH', 'OIH', 'NCH'))
        d = x.shape[-1]
        xc = jnp.transpose(x, (0, 2, 1))
        h = _bn(_conv1d(xc, conv1_w, 0), bn1_g, bn1_b, bn1_m, bn1_v)
        h = jax.nn.relu(h)
        h = _bn(_conv1d(h, conv2_w, 8), bn2_g, bn2_b, bn2_m, bn2_v)
        x_conv = jnp.transpose(jax.nn.relu(h + xc), (0, 2, 1))
        s = x @ w_se.T + b_se
        sq = jnp.sum(s * s, axis=-1)
        dist = sq[:, :, None] + sq[:, None, :] - 2.0 * jnp.einsum('bnd,bmd->bnm', s, s)
        A = jnp.exp(-dist) * mask
        msg = jax.nn.relu(x @ w_msg.T + b_msg)
        x_nmp = jnp.einsum('bnm,bmd->bnd', A, msg)
        x_in = jnp.concatenate([x_conv, x_nmp], axis=-1)
        gi = x_in @ w_ih.T + b_ih
        gh = x @ w_hh.T + b_hh
        gi_r, gi_z, gi_n = (gi[..., :d], gi[..., d:2 * d], gi[..., 2 * d:])
        gh_r, gh_z, gh_n = (gh[..., :d], gh[..., d:2 * d], gh[..., 2 * d:])
        r = jax.nn.sigmoid(gi_r + gh_r)
        z = jax.nn.sigmoid(gi_z + gh_z)
        nn_ = jnp.tanh(gi_n + r * gh_n)
        return (1.0 - z) * nn_ + z * x

    def _L1_gnn_ref(x, adj, weight, bias):
        import jax, jax.numpy as jnp
        import numpy as np
        support = jnp.einsum('bni,io->bno', x, weight)
        out = jnp.einsum('bnm,bmo->bno', adj, support)
        return out + bias
    h = jnp.maximum(_layernorm(x, axis=-1), 0.0)
    x = x + _L0_gnn_ref(h, adj, L0_gnn_w_se, L0_gnn_b_se, L0_gnn_conv1_w, L0_gnn_bn1_g, L0_gnn_bn1_b, L0_gnn_bn1_m, L0_gnn_bn1_v, L0_gnn_conv2_w, L0_gnn_bn2_g, L0_gnn_bn2_b, L0_gnn_bn2_m, L0_gnn_bn2_v, L0_gnn_w_msg, L0_gnn_b_msg, L0_gnn_w_ih, L0_gnn_b_ih, L0_gnn_w_hh, L0_gnn_b_hh)
    h = jnp.maximum(_layernorm(x, axis=-1), 0.0)
    x = x + _L1_gnn_ref(h, adj, L1_gnn_weight, L1_gnn_bias)
    return x

_drawn_inputs = setup_inputs


def setup_inputs(seed=0):
    import zlib

    import numpy as np

    out = dict(_drawn_inputs(seed))
    spreads = {'L0_gnn_b_se': (0.0, 0.8),
     'L0_gnn_bn1_g': (1.0, 0.6),
     'L0_gnn_bn1_b': (0.0, 0.404),
     'L0_gnn_bn1_m': (0.0, 0.412),
     'L0_gnn_bn1_v': (1.0, 0.6),
     'L0_gnn_bn2_g': (1.0, 0.6),
     'L0_gnn_bn2_b': (0.0, 0.532),
     'L0_gnn_bn2_m': (0.0, 0.519),
     'L0_gnn_bn2_v': (1.0, 0.6),
     'L0_gnn_b_msg': (0.0, 0.1),
     'L0_gnn_b_ih': (0.0, 0.1),
     'L0_gnn_b_hh': (0.0, 0.323)}
    factors = {'L1_gnn_bias': 2.957}
    for name, (base, spread) in spreads.items():
        noise = np.random.default_rng([zlib.crc32(name.encode()), seed]).standard_normal(out[name].shape)
        drawn = base * np.exp(spread * noise) if base else spread * noise
        out[name] = jnp.asarray(drawn.astype(out[name].dtype))
    for name, factor in factors.items():
        out[name] = (out[name] * factor).astype(out[name].dtype)
    return out
```

```python
import concourse.bass as bass
from concourse import mybir
from contextlib import ExitStack

F32 = mybir.dt.float32
F32R = mybir.dt.float32r
ALU = mybir.AluOpType
ACT = mybir.ActivationFunctionType

B, N, D = 64, 128, 128
GG = 4
W = GG * N
NG = B // GG
TAPS = 17
PAD = TAPS // 2
EPS = 1e-5
SE = 9
SE2 = 32
V_G1, V_B1, V_M1, V_V1, V_G2, V_B2, V_M2, V_V2, V_IR, V_IZ, V_IN, V_HR, V_HZ, V_HN, V_SX, V_ST, V_SA = range(17)
NV = 17
CHUNKS = ((0, 5), (5, 9), (9, 13), (13, 17))


def gnn_kernel(nc, x_in, adj_in, vec_in, early_in, conv_in, gate_in, late_in, out):
    ctx = ExitStack()
    with ctx:
        def sb(name, shape, dt=F32):
            return ctx.enter_context(nc.sbuf_tensor(name, shape, dt))

        def pb(name):
            return ctx.enter_context(nc.psum_tensor(name, [128, 512], F32))

        def sem(name):
            return ctx.enter_context(nc.semaphore(name))

        x_all = sb("x_all", [128, B * D])
        adj_all = sb("adj_all", [128, B * N])
        vec = sb("vec", [128, NV])
        early = sb("early", [128, 3 * D])
        early_hi = sb("early_hi", [128, 2 * D], F32R)
        early_lo = sb("early_lo", [128, 2 * D], F32R)
        conv = sb("conv", [128, TAPS * D])
        conv_hi = sb("conv_hi", [128, TAPS * D], F32R)
        conv_lo = sb("conv_lo", [128, TAPS * D], F32R)
        gate = conv[:, 0:9 * D]
        gate_hi = sb("gate_hi", [128, 9 * D], F32R)
        gate_lo = sb("gate_lo", [128, 9 * D], F32R)
        late = sb("late", [128, D + 2 * W])
        w_msg = early[:, 2 * D:3 * D]
        w_l1 = late[:, 0:D]
        msg_bias = late[:, D:D + W]
        l1_bias = late[:, D + W:D + 2 * W]
        neg_half = sb("neg_half", [128, GG])
        bn_var = sb("bn_var", [128, 2])
        bn_rs = sb("bn_rs", [128, 2])
        bn_a = sb("bn_a", [128, 2])
        bn_t = sb("bn_t", [128, 2])
        bn_b = sb("bn_b", [128, 2])
        rz_s = sb("rz_s", [128, 2])
        rz_b = sb("rz_b", [128, 2])
        hn_b = sb("hn_b", [128, 1])
        st1 = sb("st1", [128, GG, 6])
        mv1 = sb("mv1", [128, GG, 2])
        ve1 = sb("ve1", [128, GG])
        rs1 = sb("rs1", [128, GG])
        hn = sb("hn", [128, W])
        hT = [sb(f"hT{i}", [128, W]) for i in range(2)]
        hTb = [sb(f"hTb{i}", [128, W]) for i in range(2)]
        h_hi = [sb(f"h_hi{i}", [128, W], F32R) for i in range(2)]
        h_lo = [sb(f"h_lo{i}", [128, W], F32R) for i in range(2)]
        c1 = sb("c1", [128, GG, N])
        c1_hi = [sb(f"c1_hi{i}", [128, GG, N + 2 * PAD], F32R) for i in range(2)]
        c1_lo = [sb(f"c1_lo{i}", [128, GG, N + 2 * PAD], F32R) for i in range(2)]
        sx = sb("sx", [SE2 + SE, W])
        sy = sb("sy", [SE2 + SE, W])
        left = sb("left", [SE, W])
        right = sb("right", [SE, W])
        expd = sb("expd", [128, W])
        attT = sb("attT", [128, W])
        msg_t = sb("msg_t", [128, W])
        msg = sb("msg", [128, W])
        n_hi = [sb(f"n_hi{i}", [128, W], F32R) for i in range(2)]
        n_lo = [sb(f"n_lo{i}", [128, W], F32R) for i in range(2)]
        ct = sb("ct", [128, W])
        xc_hi = sb("xc_hi", [128, W], F32R)
        xc_lo = sb("xc_lo", [128, W], F32R)
        tr = sb("tr", [128, W])
        tz = sb("tz", [128, W])
        ghn = sb("ghn", [128, W])
        u = sb("u", [128, W])
        v = sb("v", [128, W])
        nn = sb("nn", [128, W])
        dif = sb("dif", [128, W])
        zw = sb("zw", [128, W])
        oT = sb("oT", [128, W])
        x1 = sb("x1", [128, W])
        x1b = sb("x1b", [128, W])
        st2 = sb("st2", [128, GG, 6])
        mv2 = sb("mv2", [128, GG, 2])
        ve2 = sb("ve2", [128, GG])
        rs2 = sb("rs2", [128, GG])
        hn2 = sb("hn2", [128, W])
        h2 = sb("h2", [128, W])
        uT = sb("uT", [128, W])
        ident = sb("ident", [128, 128])

        pF = pb("pF")
        pH = pb("pH")
        pC = pb("pC")
        pR, pZ, pI, pN = pb("pR"), pb("pZ"), pb("pI"), pb("pN")

        x_loaded = [sem(f"x_loaded{i}") for i in range(2)]
        adj_loaded = [sem(f"adj_loaded{i}") for i in range(2)]
        vec_loaded, early_loaded, conv_loaded, gate_loaded, late_loaded = map(
            sem, ("vec_loaded", "early_loaded", "conv_loaded", "gate_loaded", "late_loaded"))
        stored = sem("stored")
        waits_carried = [sem(f"waits_carried_{e}") for e in ("dve", "pool")]
        half_set, var_set, bnrs_set, bna_set, bnt_set, bnb_set, rzs_set, vecs_set = map(
            sem, ("half_set", "var_set", "bnrs_set", "bna_set", "bnt_set", "bnb_set", "rzs_set", "vecs_set"))
        ident_zero, ident_set, pads_set = map(sem, ("ident_zero", "ident_set", "pads_set"))
        early_rounded, early_split, conv_rounded, conv_split, gate_rounded, gate_split = map(
            sem, ("early_rounded", "early_split", "conv_rounded", "conv_split", "gate_rounded", "gate_split"))
        st1_set, mv1_set, ve1_set, rs1_set, hn_set = map(sem, ("st1_set", "mv1_set", "ve1_set", "rs1_set", "hn_set"))
        hT_placed, hT_set, hhi_set, hlo_set, hTb_set = map(
            sem, ("hT_placed", "hT_set", "hhi_set", "hlo_set", "hTb_set"))
        conv1_done, c1_set, c1hi_set, c1lo_set = map(sem, ("conv1_done", "c1_set", "c1hi_set", "c1lo_set"))
        s_done, sy_set, lr_set = map(sem, ("s_done", "sy_set", "lr_set"))
        dist_done, exp_set, att_set = map(sem, ("dist_done", "exp_set", "att_set"))
        msg_done, msgt_set, msg_set = map(sem, ("msg_done", "msgt_set", "msg_set"))
        nmp_done, nhi_set, nlo_set = map(sem, ("nmp_done", "nhi_set", "nlo_set"))
        conv2_done, ct_set, xchi_set, xclo_set = map(sem, ("conv2_done", "ct_set", "xchi_set", "xclo_set"))
        gates_done = sem("gates_done")
        ghn_set, tz_set, u_set, v_set, nn_set, dif_set, zw_set, oT_set = map(
            sem, ("ghn_set", "tz_set", "u_set", "v_set", "nn_set", "dif_set", "zw_set", "oT_set"))
        o_placed, x1_set, st2_set, mv2_set, ve2_set, rs2_set, hn2_set, h2_set, x1b_set = map(
            sem, ("o_placed", "x1_set", "st2_set", "mv2_set", "ve2_set", "rs2_set", "hn2_set", "h2_set", "x1b_set"))
        uT_done, uT_set, l1_done, out_set = map(sem, ("uT_done", "uT_set", "l1_done", "out_set"))

        def have(eng, s, n):
            if not isinstance(n, int) or n > 0:
                eng.wait_ge(s, n)

        def carry(eng):
            eng.sem_inc(waits_carried[eng is nc.gpsimd], 1)

        def steps(eng, step, first=-2):
            for t in range(first, 2):
                step(t, t // 2, t % 2)
            with eng.Fori(1, NG // 2 - 1) as u:
                step(2 * u, u, 0)
                step(2 * u + 1, u, 1)
            for t in range(NG - 2, NG + 1):
                step(t, t // 2, t % 2)

        def live(t, k=0):
            return not isinstance(t, int) or 0 <= t + k < NG

        def cols(g):
            return bass.ds(g * W, W)

        def graph(g, j):
            return bass.ds(g * W + j * N, N)

        def loaded(eng, pair, u, par, k):
            eng.wait_ge(pair[(par + k) % 2], 16 * (u + (par + k) // 2 + 1))

        block = ctx.enter_context(nc.Block())

        @block.sync
        def _(sp):
            sp.dma_start(x_all[:, 0:W], x_in[:, 0:W]).then_inc(x_loaded[0], 16)
            sp.dma_start(early[:], early_in).then_inc(early_loaded, 16)
            sp.dma_start(x_all[:, W:2 * W], x_in[:, W:2 * W]).then_inc(x_loaded[1], 16)
            sp.dma_start(conv[:], conv_in).then_inc(conv_loaded, 16)
            sp.wait_ge(conv_split, 1)
            sp.dma_start(gate, gate_in).then_inc(gate_loaded, 16)

            def load(t, u, par):
                loaded(sp, x_loaded, u, par, 2)
                loaded(sp, adj_loaded, u, par, 2)
                sp.dma_start(x_all[:, cols(t + 4)], x_in[:, cols(t + 4)]).then_inc(x_loaded[par], 16)
                sp.dma_start(adj_all[:, cols(t + 4)], adj_in[:, cols(t + 4)]).then_inc(adj_loaded[par], 16)

            def step(t, u, par):
                if live(t, 4) and not (isinstance(t, int) and t + 4 < 2):
                    load(t, u, par)
                if live(t, -1):
                    sp.wait_ge(out_set, t)
                    sp.dma_start(out[:, cols(t - 1)], x_all[:, cols(t - 1)]).then_inc(stored, 16)

            for t in range(-2, 2):
                step(t, t // 2, t % 2)
            with sp.Fori(1, NG // 2 - 2) as u:
                step(2 * u, u, 0)
                step(2 * u + 1, u, 1)
            for t in range(NG - 4, NG + 1):
                step(t, t // 2, t % 2)
            sp.wait_ge(stored, 16 * NG)

        @block.tensor
        def _(pe):
            def split_product(acc, w_hi, w_lo, m_hi, m_lo, start, stop):
                pe.matmul(acc, w_hi, m_hi, start=start, stop=False)
                pe.matmul(acc, w_hi, m_lo, start=False, stop=False)
                return pe.matmul(acc, w_lo, m_hi, start=False, stop=stop)

            def conv2_taps(par, lo, hi):
                for k in range(lo, hi):
                    last = split_product(pC[:], conv_hi[:, k * D:(k + 1) * D], conv_lo[:, k * D:(k + 1) * D],
                                         c1_hi[par][:, :, k:k + N], c1_lo[par][:, :, k:k + N],
                                         start=k == 0, stop=k == TAPS - 1)
                return last

            def gate_part(acc, part, which, m_hi, m_lo, start, stop):
                w = slice((3 * part + which) * D, (3 * part + which + 1) * D)
                return split_product(acc[:], gate_hi[:, w], gate_lo[:, w], m_hi[:], m_lo[:], start, stop)

            def step(t, u, par):
                a, g, d = t + 1, t, t - 1
                other = 1 - par
                if live(t, 1):
                    if isinstance(t, int) and t == -1:
                        pe.wait_ge(ident_set, 1)
                    have(pe, hn_set, a + 1)
                    have(pe, nlo_set, a)
                    for j in range(GG):
                        last = pe.transpose(pF[:, j * N:(j + 1) * N], hn[:, j * N:(j + 1) * N], ident[:])
                    last.then_inc(hT_placed, 1)
                if live(t):
                    if isinstance(t, int) and t == 0:
                        pe.wait_ge(conv_split, 1)
                        pe.wait_ge(pads_set, 1)
                    have(pe, c1lo_set, g + 1)
                    have(pe, ct_set, g)
                    conv2_taps(par, *CHUNKS[0])
                    conv2_taps(par, *CHUNKS[1])
                if live(t, 1):
                    if isinstance(t, int) and t == -1:
                        pe.wait_ge(early_split, 1)
                    have(pe, hlo_set, a + 1)
                    have(pe, out_set, a - 2)
                    split_product(pH[:], early_hi[:, 0:D], early_lo[:, 0:D], h_hi[other][:], h_lo[other][:],
                                  True, True).then_inc(conv1_done, 1)
                    split_product(pF[:], early_hi[:, D:2 * D], early_lo[:, D:2 * D], h_hi[other][:], h_lo[other][:],
                                  True, True).then_inc(s_done, 1)
                if live(t):
                    conv2_taps(par, *CHUNKS[2])
                if live(t, -1):
                    have(pe, oT_set, d + 1)
                    if live(t, 1):
                        have(pe, c1_set, a + 1)
                    for j in range(GG):
                        last = pe.transpose(pH[:, j * N:(j + 1) * N], oT[:, j * N:(j + 1) * N], ident[:])
                    last.then_inc(o_placed, 1)
                if live(t, 1):
                    have(pe, sy_set, a + 1)
                    for j in range(GG):
                        last = pe.matmul(pF[:, j * N:(j + 1) * N], hT[other][:, j * N:(j + 1) * N], w_msg,
                                         start=True, stop=True)
                    last.then_inc(msg_done, 1)
                if live(t):
                    conv2_taps(par, *CHUNKS[3]).then_inc(conv2_done, 1)
                if live(t, 1):
                    have(pe, lr_set, a + 1)
                    have(pe, msgt_set, a + 1)
                    for j in range(GG):
                        last = pe.matmul(pF[:, j * N:(j + 1) * N], left[:, j * N:(j + 1) * N],
                                         right[:, j * N:(j + 1) * N], start=True, stop=True)
                    last.then_inc(dist_done, 1)
                if live(t):
                    if isinstance(t, int) and t == 0:
                        pe.wait_ge(gate_split, 1)
                    have(pe, v_set, g)
                    have(pe, tz_set, g)
                    gate_part(pN, 2, 2, h_hi[par], h_lo[par], True, True)
                    gate_part(pR, 2, 0, h_hi[par], h_lo[par], True, False)
                    gate_part(pZ, 2, 1, h_hi[par], h_lo[par], True, False)
                    have(pe, nlo_set, g + 1)
                    gate_part(pR, 1, 0, n_hi[par], n_lo[par], False, False)
                    gate_part(pZ, 1, 1, n_hi[par], n_lo[par], False, False)
                    gate_part(pI, 1, 2, n_hi[par], n_lo[par], True, False)
                if live(t, -1):
                    have(pe, h2_set, d + 1)
                    for j in range(GG):
                        last = pe.matmul(pH[:, j * N:(j + 1) * N], h2[:, j * N:(j + 1) * N],
                                         adj_all[:, graph(d, j)], start=True, stop=True)
                    last.then_inc(uT_done, 1)
                if live(t):
                    have(pe, xclo_set, g + 1)
                    gate_part(pR, 0, 0, xc_hi, xc_lo, False, True)
                    gate_part(pZ, 0, 1, xc_hi, xc_lo, False, True)
                    gate_part(pI, 0, 2, xc_hi, xc_lo, False, True).then_inc(gates_done, 1)
                if live(t, 1):
                    have(pe, att_set, a + 1)
                    have(pe, msg_set, a + 1)
                    for j in range(GG):
                        last = pe.matmul(pF[:, j * N:(j + 1) * N], msg[:, j * N:(j + 1) * N],
                                         attT[:, j * N:(j + 1) * N], start=True, stop=True)
                    last.then_inc(nmp_done, 1)
                if live(t, -1):
                    have(pe, uT_set, d + 1)
                    if isinstance(t, int) and t == 1:
                        pe.wait_ge(late_loaded, 16)
                    for j in range(GG):
                        last = pe.matmul(pH[:, j * N:(j + 1) * N], uT[:, j * N:(j + 1) * N], w_l1,
                                         start=True, stop=True)
                    last.then_inc(l1_done, 1)

            steps(pe, step)

        @block.scalar
        def _(act):
            act.dma_start(vec[:], vec_in).then_inc(vec_loaded, 16)
            act.dma_start(adj_all[:, 0:W], adj_in[:, 0:W]).then_inc(adj_loaded[0], 16)
            act.dma_start(adj_all[:, W:2 * W], adj_in[:, W:2 * W]).then_inc(adj_loaded[1], 16)
            act.dma_start(late[:], late_in).then_inc(late_loaded, 16)
            act.wait_ge(vecs_set, 1)

            def step(t, u, par):
                a, g, d = t + 1, t, t - 1
                other = 1 - par
                if live(t, -1):
                    have(act, gates_done, d + 1)
                    act.activation(tr[:], pR[:], ACT.Tanh, bias=rz_b[:, 0:1], scale=0.5)
                    act.activation(ghn[:], pN[:], ACT.Identity, bias=hn_b[:, 0:1], scale=0.5).then_inc(ghn_set, 1)
                    have(act, oT_set, d)
                    act.activation(tz[:], pZ[:], ACT.Tanh, bias=rz_b[:, 1:2], scale=0.5).then_inc(tz_set, 1)
                    have(act, v_set, d + 1)
                    act.activation(nn[:], v[:], ACT.Tanh, bias=vec[:, V_IN:V_IN + 1], scale=1.0).then_inc(nn_set, 1)
                if live(t, 1):
                    have(act, hT_placed, a + 1)
                    have(act, dif_set, a - 1)
                    act.activation(hT[other][:], pF[:], ACT.Relu).then_inc(hT_set, 1)
                    have(act, conv1_done, a + 1)
                    have(act, c1lo_set, a)
                    act.activation(c1[:].rearrange("p g n -> p (g n)"), pH[:], ACT.Relu, bias=bn_b[:, 0:1],
                                   scale=bn_a[:, 0:1]).then_inc(c1_set, 1)
                    have(act, s_done, a + 1)
                    have(act, lr_set, a)
                    act.activation(sx[:], pF[0:SE2 + SE, :], ACT.Identity, bias=vec[0:SE2 + SE, V_SX:V_SX + 1],
                                   scale=1.0)
                    act.activation(sy[:], pF[0:SE2 + SE, :], ACT.Identity, bias=vec[0:SE2 + SE, V_ST:V_ST + 1],
                                   scale=vec[0:SE2 + SE, V_SA:V_SA + 1]).then_inc(sy_set, 1)
                if live(t, -1):
                    have(act, hn2_set, d + 1)
                    have(act, uT_done, d)
                    act.activation(h2[:], hn2[:], ACT.Relu).then_inc(h2_set, 1)
                if live(t, 1):
                    have(act, dist_done, a + 1)
                    have(act, att_set, a)
                    act.activation(expd[:], pF[:], ACT.Exp, scale=-1.0).then_inc(exp_set, 1)
                if live(t, -1):
                    have(act, uT_done, d + 1)
                    have(act, l1_done, d)
                    act.activation(uT[:], pH[:], ACT.Copy).then_inc(uT_set, 1)
                if live(t, 1):
                    have(act, nmp_done, a + 1)
                    act.activation(n_hi[other][:], pF[:], ACT.Copy).then_inc(nhi_set, 1)

            steps(act, step)

        @block.vector
        def _(dve):
            dve.memset(neg_half[:], -0.5).then_inc(half_set, 1)
            dve.wait_ge(vec_loaded, 16)
            dve.tensor_scalar(bn_var[:, 0:1], vec[:, V_V1:V_V1 + 1], EPS, None, ALU.add)
            dve.tensor_scalar(bn_var[:, 1:2], vec[:, V_V2:V_V2 + 1], EPS, None, ALU.add).then_inc(var_set, 1)
            dve.tensor_tensor(rz_s[:], vec[:, V_IR:V_IZ + 1], vec[:, V_HR:V_HZ + 1], ALU.add).then_inc(rzs_set, 1)
            dve.wait_ge(bnrs_set, 1)
            dve.tensor_tensor(bn_a[:, 0:1], bn_rs[:, 0:1], vec[:, V_G1:V_G1 + 1], ALU.mult)
            dve.tensor_tensor(bn_a[:, 1:2], bn_rs[:, 1:2], vec[:, V_G2:V_G2 + 1], ALU.mult).then_inc(bna_set, 1)
            dve.wait_ge(bna_set, 1)
            dve.tensor_tensor(bn_t[:, 0:1], bn_a[:, 0:1], vec[:, V_M1:V_M1 + 1], ALU.mult)
            dve.tensor_tensor(bn_t[:, 1:2], bn_a[:, 1:2], vec[:, V_M2:V_M2 + 1], ALU.mult).then_inc(bnt_set, 1)
            dve.wait_ge(bnt_set, 1)
            dve.tensor_tensor(bn_b[:, 0:1], vec[:, V_B1:V_B1 + 1], bn_t[:, 0:1], ALU.subtract)
            dve.tensor_tensor(bn_b[:, 1:2], vec[:, V_B2:V_B2 + 1], bn_t[:, 1:2], ALU.subtract)
            dve.wait_ge(rzs_set, 1)
            dve.tensor_scalar(rz_b[:], rz_s[:], 0.5, None, ALU.mult)
            dve.tensor_scalar(hn_b[:], vec[:, V_HN:V_HN + 1], 0.5, None, ALU.mult).then_inc(vecs_set, 1)
            for buf in (*c1_hi, *c1_lo):
                dve.memset(buf[:, :, 0:PAD].bitcast(F32), 0.0)
                last = dve.memset(buf[:, :, PAD + N:2 * PAD + N].bitcast(F32), 0.0)
            last.then_inc(pads_set, 1)

            def split(whole, hi, lo, rounded, done):
                dve.tensor_copy(hi, whole).then_inc(rounded, 1)
                dve.wait_ge(rounded, 1)
                dve.tensor_tensor(lo, whole, hi.bitcast(F32), ALU.subtract).then_inc(done, 1)

            def normalise1(t, u, par):
                b = t + 2
                loaded(dve, x_loaded, u, par, 2)
                for j in range(GG):
                    last = dve.bn_stats(st1[:, j, :], x_all[:, graph(b, j)])
                last.then_inc(st1_set, 1)
                have(dve, st1_set, b + 1)
                carry(dve)
                for j in range(GG):
                    last = dve.bn_aggr(mv1[:, j, :], st1[:, j, :])
                last.then_inc(mv1_set, 1)
                have(dve, mv1_set, b + 1)
                dve.tensor_scalar(ve1[:], mv1[:, :, 1], EPS, None, ALU.add).then_inc(ve1_set, 1)

            def apply1(t):
                b = t + 2
                have(dve, rs1_set, b + 1)
                have(dve, hT_placed, b)
                for j in range(GG):
                    last = dve.tensor_scalar(hn[:, j * N:(j + 1) * N], x_all[:, graph(b, j)], mv1[:, j, 0:1],
                                             rs1[:, j:j + 1], ALU.subtract, ALU.mult)
                last.then_inc(hn_set, 1)

            def step(t, u, par):
                a, g, d = t + 1, t, t - 1
                other = 1 - par
                if live(t, -1):
                    have(dve, ghn_set, d + 1)
                    dve.scalar_tensor_tensor(u_[:], tr[:], 1.0, ghn[:], ALU.add, ALU.mult).then_inc(u_set, 1)
                    have(dve, u_set, d + 1)
                    dve.tensor_tensor(v[:], pI[:], u_[:], ALU.add).then_inc(v_set, 1)
                    have(dve, dif_set, d + 1)
                    dve.scalar_tensor_tensor(zw[:], tz[:], 1.0, dif[:], ALU.add, ALU.mult).then_inc(zw_set, 1)
                    have(dve, zw_set, d + 1)
                    have(dve, o_placed, d)
                    dve.scalar_tensor_tensor(oT[:], zw[:], 0.5, nn[:], ALU.mult, ALU.add).then_inc(oT_set, 1)
                if live(t, 2):
                    normalise1(t, u, par)
                if isinstance(t, int) and t == -2:
                    apply1(t)
                    dve.wait_ge(early_loaded, 16)
                    split(early[:, 0:2 * D], early_hi[:], early_lo[:], early_rounded, early_split)
                if live(t, 1):
                    have(dve, sy_set, a + 1)
                    have(dve, dist_done, a)
                    dve.tensor_tensor(left[:], sx[0:SE, :], sy[0:SE, :], ALU.mult)
                    dve.tensor_tensor(right[:], sx[SE2:SE2 + SE, :], sy[SE2:SE2 + SE, :], ALU.mult).then_inc(lr_set, 1)
                if live(t, 2) and not (isinstance(t, int) and t == -2):
                    apply1(t)
                if isinstance(t, int) and t == -1:
                    dve.wait_ge(conv_loaded, 16)
                    split(conv[:], conv_hi[:], conv_lo[:], conv_rounded, conv_split)
                if live(t, -1):
                    have(dve, o_placed, d + 1)
                    have(dve, x1b_set, d)
                    dve.tensor_tensor(x1[:], pH[:], x_all[:, cols(d)], ALU.add).then_inc(x1_set, 1)
                    have(dve, x1_set, d + 1)
                    for j in range(GG):
                        last = dve.bn_stats(st2[:, j, :], x1[:, j * N:(j + 1) * N])
                    last.then_inc(st2_set, 1)
                    have(dve, st2_set, d + 1)
                    carry(dve)
                    for j in range(GG):
                        last = dve.bn_aggr(mv2[:, j, :], st2[:, j, :])
                    last.then_inc(mv2_set, 1)
                    have(dve, mv2_set, d + 1)
                    dve.tensor_scalar(ve2[:], mv2[:, :, 1], EPS, None, ALU.add).then_inc(ve2_set, 1)
                if live(t, 1):
                    if isinstance(t, int) and t == -1:
                        dve.wait_ge(late_loaded, 16)
                    have(dve, msg_done, a + 1)
                    have(dve, msg_set, a)
                    dve.tensor_tensor(msg_t[:], pF[:], msg_bias, ALU.add).then_inc(msgt_set, 1)
                if live(t, -1):
                    have(dve, rs2_set, d + 1)
                    have(dve, h2_set, d)
                    for j in range(GG):
                        last = dve.tensor_scalar(hn2[:, j * N:(j + 1) * N], x1[:, j * N:(j + 1) * N],
                                                 mv2[:, j, 0:1], rs2[:, j:j + 1], ALU.subtract, ALU.mult)
                    last.then_inc(hn2_set, 1)
                if live(t):
                    have(dve, conv2_done, g + 1)
                    have(dve, hTb_set, g + 1)
                    dve.scalar_tensor_tensor(ct[:], pC[:], bn_a[:, 1:2], hTb[par][:], ALU.mult, ALU.add)\
                       .then_inc(ct_set, 1)
                    have(dve, ct_set, g + 1)
                    have(dve, gates_done, g)
                    dve.tensor_scalar(xc_hi[:], ct[:], 0.0, None, ALU.max).then_inc(xchi_set, 1)
                    have(dve, xchi_set, g + 1)
                    dve.scalar_tensor_tensor(xc_lo[:], ct[:], 0.0, xc_hi[:].bitcast(F32), ALU.max, ALU.subtract)\
                       .then_inc(xclo_set, 1)
                if live(t, 1):
                    loaded(dve, adj_loaded, u, par, 1)
                    have(dve, exp_set, a + 1)
                    have(dve, nmp_done, a)
                    dve.tensor_tensor(attT[:], expd[:], adj_all[:, cols(a)], ALU.mult).then_inc(att_set, 1)
                if isinstance(t, int) and t == -1:
                    dve.wait_ge(gate_loaded, 16)
                    split(gate, gate_hi[:], gate_lo[:], gate_rounded, gate_split)
                if live(t, 1):
                    have(dve, nhi_set, a + 1)
                    dve.tensor_tensor(n_lo[other][:], pF[:], n_hi[other][:].bitcast(F32), ALU.subtract)\
                       .then_inc(nlo_set, 1)
                if live(t, -1):
                    have(dve, l1_done, d + 1)
                    have(dve, x1b_set, d + 1)
                    dve.tensor_tensor(x_all[:, cols(d)], pH[:], x1b[:], ALU.add).then_inc(out_set, 1)

            u_ = u
            steps(dve, step)

        @block.gpsimd
        def _(pool):
            pool.memset(ident[:], 0.0).then_inc(ident_zero, 1)
            pool.wait_ge(ident_zero, 1)
            pool.affine_select(out=ident[:], in_=ident[:], compare_op=ALU.not_equal, fill=1.0, base=0,
                               pattern=[[-1, 128]], channel_multiplier=1).then_inc(ident_set, 1)
            pool.wait_ge(half_set, 1)
            pool.wait_ge(var_set, 1)
            pool.tensor_tensor(bn_rs[:], bn_var[:], neg_half[:, 0:2], ALU.pow).then_inc(bnrs_set, 1)
            pool.wait_ge(vecs_set, 1)

            def step(t, u, par):
                a, d = t + 1, t - 1
                other = 1 - par
                if live(t, -1):
                    have(pool, nn_set, d + 1)
                    have(pool, zw_set, d)
                    pool.tensor_tensor(dif[:], hT[other][:], nn[:], ALU.subtract).then_inc(dif_set, 1)
                if live(t, 2) and isinstance(t, int) and t == -2:
                    have(pool, ve1_set, t + 3)
                    pool.tensor_tensor(rs1[:], ve1[:], neg_half[:], ALU.pow).then_inc(rs1_set, 1)
                if live(t, 1):
                    have(pool, hT_set, a + 1)
                    carry(pool)
                    pool.tensor_scalar(h_hi[other][:], hT[other][:], 1.0, 0.0, ALU.mult, ALU.add).then_inc(hhi_set, 1)
                    have(pool, hhi_set, a + 1)
                    pool.tensor_tensor(h_lo[other][:], hT[other][:], h_hi[other][:].bitcast(F32), ALU.subtract)\
                        .then_inc(hlo_set, 1)
                if live(t, 2) and not (isinstance(t, int) and t == -2):
                    have(pool, ve1_set, t + 3)
                    have(pool, hn_set, t + 2)
                    pool.tensor_tensor(rs1[:], ve1[:], neg_half[:], ALU.pow).then_inc(rs1_set, 1)
                if live(t, 1):
                    have(pool, c1_set, a + 1)
                    have(pool, conv2_done, a - 1)
                    carry(pool)
                    pool.tensor_scalar(c1_hi[other][:, :, PAD:PAD + N], c1[:], 1.0, 0.0, ALU.mult, ALU.add)\
                        .then_inc(c1hi_set, 1)
                    have(pool, c1hi_set, a + 1)
                    pool.tensor_tensor(c1_lo[other][:, :, PAD:PAD + N], c1[:],
                                       c1_hi[other][:, :, PAD:PAD + N].bitcast(F32), ALU.subtract)\
                        .then_inc(c1lo_set, 1)
                    have(pool, ct_set, a - 1)
                    carry(pool)
                    pool.tensor_scalar(hTb[other][:], hT[other][:], bn_b[:, 1:2], 1.0, ALU.add, ALU.mult)\
                        .then_inc(hTb_set, 1)
                if live(t, -1):
                    have(pool, ve2_set, d + 1)
                    pool.tensor_tensor(rs2[:], ve2[:], neg_half[:], ALU.pow).then_inc(rs2_set, 1)
                if live(t, 1):
                    have(pool, msgt_set, a + 1)
                    have(pool, nmp_done, a)
                    carry(pool)
                    pool.tensor_scalar(msg[:], msg_t[:], 0.0, 0.0, ALU.max, ALU.add).then_inc(msg_set, 1)
                if live(t, -1):
                    if isinstance(t, int) and t == 1:
                        pool.wait_ge(late_loaded, 16)
                    have(pool, out_set, d)
                    pool.tensor_tensor(x1b[:], x1[:], l1_bias, ALU.add).then_inc(x1b_set, 1)

            steps(pool, step)


def kernel(**inputs):
    import numpy as np
    import concourse.bacc as bacc
    from concourse.bass_utils import run_bass_kernel_spmd

    p = {k: np.asarray(v) for k, v in inputs.items()}
    f = {k.removeprefix("L0_gnn_"): v for k, v in p.items()}
    one, zero = np.ones(3, np.float32), np.zeros(3, np.float32)
    gap = np.zeros(SE2 - SE, np.float32)
    tail = np.zeros(128 - SE2 - SE, np.float32)
    b_se, w_se = f["b_se"], f["w_se"].T
    zw = np.zeros((D, 3), np.float32)
    se_x = np.concatenate([b_se, b_se, one, gap, b_se, one, b_se, tail])
    se_t = np.concatenate([one, b_se, one, gap, -2 * one, one, b_se, tail])
    se_a = np.concatenate([zero, one, zero, gap, zero, zero, one, tail])
    w_s = np.concatenate([w_se, w_se, zw, np.zeros((D, SE2 - SE), np.float32), w_se, zw, w_se,
                          np.zeros((D, 128 - SE2 - SE), np.float32)], axis=1)
    vec = np.stack([f["bn1_g"], f["bn1_b"], f["bn1_m"], f["bn1_v"], f["bn2_g"], f["bn2_b"], f["bn2_m"], f["bn2_v"],
                    *f["b_ih"].reshape(3, D), *f["b_hh"].reshape(3, D), se_x, se_t, se_a], axis=1)
    rows = lambda b: np.broadcast_to(np.tile(b, GG), (128, W))
    arrays = {
        "x_in": p["x"].transpose(1, 0, 2).reshape(N, B * D),
        "adj_in": p["adj"].transpose(2, 0, 1).reshape(N, B * N),
        "vec_in": vec,
        "early_in": np.concatenate([f["conv1_w"][:, :, 0].T, w_s, f["w_msg"].T], axis=1),
        "conv_in": f["conv2_w"].transpose(1, 2, 0).reshape(D, TAPS * D),
        "gate_in": np.concatenate([f["w_ih"][:, 0:D].T, f["w_ih"][:, D:2 * D].T, f["w_hh"].T], axis=1),
        "late_in": np.concatenate([p["L1_gnn_weight"], rows(f["b_msg"]), rows(p["L1_gnn_bias"])], axis=1),
    }
    arrays = {k: np.ascontiguousarray(a) for k, a in arrays.items()}
    nc = bacc.Bacc("TRN2", target_bir_lowering=False, num_devices=1)
    args = [nc.dram_tensor(k, a.shape, F32, kind="ExternalInput").ap() for k, a in arrays.items()]
    out = nc.dram_tensor("out", (N, B * D), F32, kind="ExternalOutput").ap()
    gnn_kernel(nc, *args, out)
    r = run_bass_kernel_spmd(nc, [arrays], core_ids=[0])
    return r.results[0]["out"].reshape(N, B, D).transpose(1, 0, 2)
```

```python
import concourse.bass as bass
from concourse import mybir
from contextlib import ExitStack

F32 = mybir.dt.float32
F32R = mybir.dt.float32r
ALU = mybir.AluOpType
ACT = mybir.ActivationFunctionType

B, N, D = 64, 128, 128
GG = 4
W = GG * N
NG = B // GG
TAPS = 17
PAD = TAPS // 2
EPS = 1e-5
SE = 9
SE2 = 32
V_G1, V_B1, V_M1, V_V1, V_G2, V_B2, V_M2, V_V2, V_IR, V_IZ, V_IN, V_HR, V_HZ, V_HN, V_SX, V_ST, V_SA = range(17)
NV = 17
HALF = N // 2
TE, TO = (TAPS + 1) // 2, TAPS // 2
HA = HALF + 2
PW = HALF + TE + 2
PE0, PO0 = PAD // 2, PAD // 2 + 1


def gnn_kernel(nc, x_in, adj_in, vec_in, early_in, conv_in, gate_in, late_in, out):
    ctx = ExitStack()
    with ctx:
        def sb(name, shape, dt=F32):
            return ctx.enter_context(nc.sbuf_tensor(name, shape, dt))

        def pb(name):
            return ctx.enter_context(nc.psum_tensor(name, [128, 512], F32))

        def sem(name):
            return ctx.enter_context(nc.semaphore(name))

        x_all = sb("x_all", [128, B * D])
        adj_all = sb("adj_all", [128, B * N])
        vec = sb("vec", [128, NV])
        early = sb("early", [128, 3 * D])
        early_hi = sb("early_hi", [128, 2 * D], F32R)
        early_lo = sb("early_lo", [128, 2 * D], F32R)
        conv = x_all[:, B * D - (TAPS + TO) * D:]
        conv_hi = sb("conv_hi", [128, (TAPS + TO) * D], F32R)
        conv_lo = sb("conv_lo", [128, (TAPS + TO) * D], F32R)
        gate = x_all[:, B * D - (TAPS + TO + 9) * D:B * D - (TAPS + TO) * D]
        gate_hi = sb("gate_hi", [128, 9 * D], F32R)
        gate_lo = sb("gate_lo", [128, 9 * D], F32R)
        late = sb("late", [128, D + 2 * W])
        w_msg = early[:, 2 * D:3 * D]
        w_l1 = late[:, 0:D]
        msg_bias = late[:, D:D + W]
        l1_bias = late[:, D + W:D + 2 * W]
        neg_half = sb("neg_half", [128, GG])
        warm = sb("warm", [128, 1])
        bn_var = sb("bn_var", [128, 2])
        bn_rs = sb("bn_rs", [128, 2])
        bn_a = sb("bn_a", [128, 2])
        bn_t = sb("bn_t", [128, 2])
        bn_b = sb("bn_b", [128, 2])
        neg_a2 = sb("neg_a2", [128, 1])
        rz_s = sb("rz_s", [128, 2])
        rz_b = sb("rz_b", [128, 2])
        hn_b = sb("hn_b", [128, 1])
        st1 = sb("st1", [128, GG, 6])
        mv1 = sb("mv1", [128, GG, 2])
        ve1 = sb("ve1", [128, GG])
        rs1 = sb("rs1", [128, GG])
        hn = sb("hn", [128, W])
        hT = [sb(f"hT{i}", [128, W]) for i in range(2)]
        hTb = [sb(f"hTb{i}", [128, W]) for i in range(2)]
        h_hi = [sb(f"h_hi{i}", [128, W], F32R) for i in range(2)]
        h_lo = [sb(f"h_lo{i}", [128, W], F32R) for i in range(2)]
        c1 = sb("c1", [128, 3, GG, PW])
        c1_hi = [sb(f"c1_hi{i}", [128, 3, GG, PW], F32R) for i in range(2)]
        c1_lo = [sb(f"c1_lo{i}", [128, 3, GG, PW], F32R) for i in range(2)]
        sx = sb("sx", [SE2 + SE, W])
        sy = sb("sy", [SE2 + SE, W])
        left = sb("left", [SE, W])
        right = sb("right", [SE, W])
        expd = sb("expd", [128, W])
        attT = sb("attT", [128, W])
        msg_t = sb("msg_t", [128, W])
        msg = sb("msg", [128, W])
        n_hi = [sb(f"n_hi{i}", [128, W], F32R) for i in range(2)]
        n_lo = [sb(f"n_lo{i}", [128, W], F32R) for i in range(2)]
        A2 = sb("A2", [128, GG, HA])
        base_e = sb("base_e", [128, GG, HALF])
        base_o = sb("base_o", [128, GG, HALF])
        odd = sb("odd", [128, GG, HALF])
        ct = sb("ct", [128, W])
        xc_hi = sb("xc_hi", [128, W], F32R)
        xc_lo = sb("xc_lo", [128, W], F32R)
        tr = sb("tr", [128, W])
        tz = sb("tz", [128, W])
        ghn = sb("ghn", [128, W])
        rh = sb("rh", [128, W])
        v = sb("v", [128, W])
        nn = sb("nn", [128, W])
        zh = sb("zh", [128, W])
        zn = sb("zn", [128, W])
        oT = sb("oT", [128, W])
        x1 = sb("x1", [128, W])
        x1b = sb("x1b", [128, W])
        st2 = sb("st2", [128, GG, 6])
        mv2 = sb("mv2", [128, GG, 2])
        ve2 = sb("ve2", [128, GG])
        rs2 = sb("rs2", [128, GG])
        hn2 = sb("hn2", [128, W])
        h2 = sb("h2", [128, W])
        uT = sb("uT", [128, W])
        ident = sb("ident", [128, 128])

        pF = pb("pF")
        pH = pb("pH")
        pA, pBC = pb("pA"), pb("pBC")
        pR, pZ, pI, pN = pb("pR"), pb("pZ"), pb("pI"), pb("pN")

        x_loaded = [sem(f"x_loaded{i}") for i in range(2)]
        adj_loaded = [sem(f"adj_loaded{i}") for i in range(2)]
        vec_loaded, early_loaded, conv_loaded, gate_loaded, late_loaded = map(
            sem, ("vec_loaded", "early_loaded", "conv_loaded", "gate_loaded", "late_loaded"))
        stored = sem("stored")
        waits_carried = [sem(f"waits_carried_{e}") for e in ("dve", "pool")]
        half_set, var_set, bnrs_set, bna_set, bnt_set, bnb_set, rzs_set, vecs_set = map(
            sem, ("half_set", "var_set", "bnrs_set", "bna_set", "bnt_set", "bnb_set", "rzs_set", "vecs_set"))
        ident_zero, ident_set, pads_set = map(sem, ("ident_zero", "ident_set", "pads_set"))
        early_rounded, early_split, conv_rounded, conv_split, sum_set, gate_rounded, gate_split = map(
            sem, ("early_rounded", "early_split", "conv_rounded", "conv_split", "sum_set", "gate_rounded", "gate_split"))
        st1_set, mv1_set, ve1_set, rs1_set, hn_set = map(sem, ("st1_set", "mv1_set", "ve1_set", "rs1_set", "hn_set"))
        hT_placed, hT_set, hhi_set, hlo_set, hTb_set = map(
            sem, ("hT_placed", "hT_set", "hhi_set", "hlo_set", "hTb_set"))
        conv1_done, c1_set, c1sum_set, c1hi_set, c1lo_set = map(
            sem, ("conv1_done", "c1_set", "c1sum_set", "c1hi_set", "c1lo_set"))
        s_done, sy_set, lr_set = map(sem, ("s_done", "sy_set", "lr_set"))
        dist_done, exp_set, att_set = map(sem, ("dist_done", "exp_set", "att_set"))
        msg_done, msgt_set, msg_set = map(sem, ("msg_done", "msgt_set", "msg_set"))
        nmp_done, nhi_set, nlo_set = map(sem, ("nmp_done", "nhi_set", "nlo_set"))
        convA_done, A2_set, base_set, conv2_done, odd_set, ct_set, xchi_set, xclo_set = map(
            sem, ("convA_done", "A2_set", "base_set", "conv2_done", "odd_set", "ct_set", "xchi_set", "xclo_set"))
        gates_done = sem("gates_done")
        ghn_set, tz_set, u_set, v_set, nn_set, zh_set, zn_set, oT_set = map(
            sem, ("ghn_set", "tz_set", "u_set", "v_set", "nn_set", "zh_set", "zn_set", "oT_set"))
        o_placed, x1_set, st2_set, mv2_set, ve2_set, rs2_set, hn2_set, h2_set, x1b_set = map(
            sem, ("o_placed", "x1_set", "st2_set", "mv2_set", "ve2_set", "rs2_set", "hn2_set", "h2_set", "x1b_set"))
        uT_done, uT_set, l1_done, out_set = map(sem, ("uT_done", "uT_set", "l1_done", "out_set"))

        def have(eng, s, n):
            if not isinstance(n, int) or n > 0:
                eng.wait_ge(s, n)

        def carry(eng):
            eng.sem_inc(waits_carried[eng is nc.gpsimd], 1)

        def steps(eng, step):
            for t in range(-1, 2):
                step(t, t // 2, t % 2)
            with eng.Fori(1, NG // 2 - 1) as u:
                step(2 * u, u, 0)
                step(2 * u + 1, u, 1)
            for t in range(NG - 2, NG + 1):
                step(t, t // 2, t % 2)

        def live(t, k=0):
            return not isinstance(t, int) or 0 <= t + k < NG

        def conv_part(n, whose=conv):
            return whose[:, (0, TE * D, TAPS * D)[n]:(TE * D, TAPS * D, (TAPS + TO) * D)[n]]

        def cols(g):
            return bass.ds(g * W, W)

        def graph(g, j):
            return bass.ds(g * W + j * N, N)

        def loaded(eng, pair, u, par, k):
            eng.wait_ge(pair[(par + k) % 2], 16 * (u + (par + k) // 2 + 1))

        block = ctx.enter_context(nc.Block())

        @block.sync
        def _(sp):
            sp.dma_start(x_all[:, 0:W], x_in[:, 0:W]).then_inc(x_loaded[0], 16)
            sp.dma_start(early[:], early_in).then_inc(early_loaded, 16)
            sp.dma_start(x_all[:, W:2 * W], x_in[:, W:2 * W]).then_inc(x_loaded[1], 16)
            sp.dma_start(conv[:, 0:TAPS * D], conv_in).then_inc(conv_loaded, 16)
            sp.dma_start(gate, gate_in).then_inc(gate_loaded, 16)

            def load(t, u, par):
                loaded(sp, x_loaded, u, par, 2)
                loaded(sp, adj_loaded, u, par, 2)
                sp.dma_start(x_all[:, cols(t + 4)], x_in[:, cols(t + 4)]).then_inc(x_loaded[par], 16)
                sp.dma_start(adj_all[:, cols(t + 4)], adj_in[:, cols(t + 4)]).then_inc(adj_loaded[par], 16)

            def step(t, u, par):
                if live(t, 4) and not (isinstance(t, int) and t + 4 < 2):
                    load(t, u, par)
                if live(t, -1):
                    sp.wait_ge(out_set, t)
                    sp.dma_start(out[:, cols(t - 1)], x_all[:, cols(t - 1)]).then_inc(stored, 16)

            for t in range(-2, 2):
                step(t, t // 2, t % 2)
            sp.wait_ge(gate_split, 1)
            with sp.Fori(1, NG // 2 - 2) as u:
                step(2 * u, u, 0)
                step(2 * u + 1, u, 1)
            for t in range(NG - 4, NG + 1):
                step(t, t // 2, t % 2)
            sp.wait_ge(stored, 16 * NG)

        @block.tensor
        def _(pe):
            def split_product(acc, w_hi, w_lo, m_hi, m_lo, start, stop):
                pe.matmul(acc, w_hi, m_hi, start=start, stop=False)
                pe.matmul(acc, w_hi, m_lo, start=False, stop=False)
                return pe.matmul(acc, w_lo, m_hi, start=False, stop=stop)

            def conv2_taps(par, product, lo, hi):
                taps = TO if product == 1 else TE
                acc = (pA[:, 0:GG * HA], pBC[:, 0:W // 2], pBC[:, W // 2:W])[product]
                start, width = ((0, HA), (1, HALF), (1, HALF))[product]
                for k in range(lo, hi):
                    w = k if product == 0 or k == TO and product == 2 else (TE + k if product == 1 else TAPS + k)
                    last = split_product(acc, conv_hi[:, w * D:(w + 1) * D], conv_lo[:, w * D:(w + 1) * D],
                                         c1_hi[par][:, product, :, start + k:start + k + width],
                                         c1_lo[par][:, product, :, start + k:start + k + width],
                                         start=k == 0, stop=k == taps - 1)
                return last

            def gate_part(acc, part, which, m_hi, m_lo, start, stop):
                w = slice((3 * part + which) * D, (3 * part + which + 1) * D)
                return split_product(acc[:], gate_hi[:, w], gate_lo[:, w], m_hi[:], m_lo[:], start, stop)

            def step(t, u, par):
                a, g, d = t + 1, t, t - 1
                other = 1 - par
                def conv_a():
                    if t_is(0):
                        pe.wait_ge(conv_split, 1)
                    have(pe, c1lo_set, g + 1)
                    have(pe, A2_set, g)
                    conv2_taps(par, 0, 0, TE).then_inc(convA_done, 1)

                def conv_b():
                    if t_is(0):
                        pe.wait_ge(conv_split, 2)
                    have(pe, ct_set, g)
                    conv2_taps(par, 1, 0, TO)

                def conv_c1():
                    if t_is(0):
                        pe.wait_ge(conv_split, 3)
                    conv2_taps(par, 2, 0, 4)

                def conv_c2():
                    conv2_taps(par, 2, 4, TE).then_inc(conv2_done, 1)

                def x_turn(q):
                    if t_is(-1):
                        pe.wait_ge(ident_set, 1)
                    have(pe, hn_set, q + 1)
                    have(pe, nlo_set, q)
                    for j in range(GG):
                        last = pe.transpose(pF[:, j * N:(j + 1) * N], hn[:, j * N:(j + 1) * N], ident[:])
                    last.then_inc(hT_placed, 1)

                def conv1_and_s(q, p):
                    if t_is(-1):
                        pe.wait_ge(early_split, 1)
                    have(pe, hlo_set, q + 1)
                    have(pe, out_set, q - 2)
                    split_product(pH[:], early_hi[:, 0:D], early_lo[:, 0:D], h_hi[p][:], h_lo[p][:],
                                  True, True).then_inc(conv1_done, 1)
                    split_product(pF[:], early_hi[:, D:2 * D], early_lo[:, D:2 * D], h_hi[p][:], h_lo[p][:],
                                  True, True).then_inc(s_done, 1)

                def messages(q, p):
                    have(pe, sy_set, q + 1)
                    for j in range(GG):
                        last = pe.matmul(pF[:, j * N:(j + 1) * N], hT[p][:, j * N:(j + 1) * N], w_msg,
                                         start=True, stop=True)
                    last.then_inc(msg_done, 1)

                def distances(q):
                    have(pe, lr_set, q + 1)
                    have(pe, msgt_set, q + 1)
                    for j in range(GG):
                        last = pe.matmul(pF[:, j * N:(j + 1) * N], left[:, j * N:(j + 1) * N],
                                         right[:, j * N:(j + 1) * N], start=True, stop=True)
                    last.then_inc(dist_done, 1)

                def neighbour_sums(q):
                    have(pe, att_set, q + 1)
                    have(pe, msg_set, q + 1)
                    for j in range(GG):
                        last = pe.matmul(pF[:, j * N:(j + 1) * N], msg[:, j * N:(j + 1) * N],
                                         attT[:, j * N:(j + 1) * N], start=True, stop=True)
                    last.then_inc(nmp_done, 1)

                def gates_h():
                    if t_is(0):
                        pe.wait_ge(gate_split, 1)
                    have(pe, v_set, g)
                    have(pe, tz_set, g)
                    gate_part(pN, 2, 2, h_hi[par], h_lo[par], True, True)
                    gate_part(pR, 2, 0, h_hi[par], h_lo[par], True, False)
                    gate_part(pZ, 2, 1, h_hi[par], h_lo[par], True, False)

                def gates_n():
                    have(pe, nlo_set, g + 1)
                    gate_part(pR, 1, 0, n_hi[par], n_lo[par], False, False)
                    gate_part(pZ, 1, 1, n_hi[par], n_lo[par], False, False)
                    gate_part(pI, 1, 2, n_hi[par], n_lo[par], True, False)

                def gates_c():
                    have(pe, xclo_set, g + 1)
                    gate_part(pR, 0, 0, xc_hi, xc_lo, False, True)
                    gate_part(pZ, 0, 1, xc_hi, xc_lo, False, True)
                    gate_part(pI, 0, 2, xc_hi, xc_lo, False, True).then_inc(gates_done, 1)

                def o_turn():
                    have(pe, oT_set, d + 1)
                    if live(t, 1):
                        have(pe, c1_set, a + 1)
                    else:
                        have(pe, out_set, d)
                    for j in range(GG):
                        last = pe.transpose(pH[:, j * N:(j + 1) * N], oT[:, j * N:(j + 1) * N], ident[:])
                    last.then_inc(o_placed, 1)

                def adj_h2():
                    have(pe, h2_set, d + 1)
                    for j in range(GG):
                        last = pe.matmul(pH[:, j * N:(j + 1) * N], h2[:, j * N:(j + 1) * N],
                                         adj_all[:, graph(d, j)], start=True, stop=True)
                    last.then_inc(uT_done, 1)

                def layer2():
                    have(pe, uT_set, d + 1)
                    if t_is(1):
                        pe.wait_ge(late_loaded, 16)
                    for j in range(GG):
                        last = pe.matmul(pH[:, j * N:(j + 1) * N], uT[:, j * N:(j + 1) * N], w_l1,
                                         start=True, stop=True)
                    last.then_inc(l1_done, 1)

                def t_is(n):
                    return isinstance(t, int) and t == n

                front, middle, back = live(t, 1), live(t), live(t, -1)
                if t_is(-1):
                    x_turn(a)
                    conv1_and_s(a, other)
                    messages(a, other)
                    return
                if t_is(0):
                    conv_a()
                    distances(g)
                    conv_b()
                    neighbour_sums(g)
                    conv_c1()
                    x_turn(a)
                    conv_c2()
                    conv1_and_s(a, other)
                    gates_h()
                    messages(a, other)
                    gates_n()
                    distances(a)
                    gates_c()
                    neighbour_sums(a)
                    return
                if middle:
                    conv_a()
                if front:
                    x_turn(a)
                if middle:
                    conv_b()
                if front:
                    conv1_and_s(a, other)
                if middle:
                    conv_c1()
                if back:
                    o_turn()
                if front:
                    messages(a, other)
                if middle:
                    conv_c2()
                    gates_h()
                if front:
                    distances(a)
                if middle:
                    gates_n()
                if middle:
                    gates_c()
                if back:
                    adj_h2()
                if front:
                    neighbour_sums(a)
                if back:
                    layer2()

            steps(pe, step)

        @block.scalar
        def _(act):
            act.dma_start(vec[:], vec_in).then_inc(vec_loaded, 16)
            act.dma_start(adj_all[:, 0:W], adj_in[:, 0:W]).then_inc(adj_loaded[0], 16)
            act.dma_start(adj_all[:, W:2 * W], adj_in[:, W:2 * W]).then_inc(adj_loaded[1], 16)
            act.dma_start(late[:], late_in).then_inc(late_loaded, 16)
            act.wait_ge(half_set, 1)
            act.activation(warm[:], neg_half[:, 0:1], ACT.Tanh)

            def step(t, u, par):
                a, g, d = t + 1, t, t - 1
                other = 1 - par
                if live(t):
                    have(act, convA_done, g + 1)
                    have(act, base_set, g)
                    act.activation(A2[:].rearrange("p g m -> p (g m)"), pA[:, 0:GG * HA], ACT.Identity, bias=0.0,
                                   scale=bn_a[:, 1:2]).then_inc(A2_set, 1)
                if live(t, 1):
                    have(act, hT_placed, a + 1)
                    have(act, zh_set, a - 1)
                    act.activation(hT[other][:], pF[:], ACT.Relu).then_inc(hT_set, 1)
                    if isinstance(t, int) and t == -1:
                        act.wait_ge(conv_loaded, 16)
                        act.activation(conv_part(0, conv_hi), conv_part(0), ACT.Copy).then_inc(conv_rounded, 1)
                        act.wait_ge(pads_set, 1)
                        act.wait_ge(vecs_set, 1)
                    have(act, conv1_done, a + 1)
                    have(act, c1lo_set, a)
                    nodes = pH[:].rearrange("p (g m two) -> p g m two", g=GG, two=2)
                    act.activation(c1[:, 0, :, PE0:PE0 + HALF], nodes[:, :, :, 0], ACT.Relu, bias=bn_b[:, 0:1],
                                   scale=bn_a[:, 0:1])
                    act.activation(c1[:, 1, :, PO0:PO0 + HALF], nodes[:, :, :, 1], ACT.Relu, bias=bn_b[:, 0:1],
                                   scale=bn_a[:, 0:1]).then_inc(c1_set, 1)
                    have(act, s_done, a + 1)
                    have(act, lr_set, a)
                    act.activation(sx[:], pF[0:SE2 + SE, :], ACT.Identity, bias=vec[0:SE2 + SE, V_SX:V_SX + 1],
                                   scale=1.0)
                    act.activation(sy[:], pF[0:SE2 + SE, :], ACT.Identity, bias=vec[0:SE2 + SE, V_ST:V_ST + 1],
                                   scale=vec[0:SE2 + SE, V_SA:V_SA + 1]).then_inc(sy_set, 1)
                    if isinstance(t, int) and t == -1:
                        act.activation(conv_part(1, conv_hi), conv_part(1), ACT.Copy).then_inc(conv_rounded, 1)
                    have(act, msgt_set, a + 1)
                    have(act, nmp_done, a)
                    act.activation(msg[:], msg_t[:], ACT.Relu).then_inc(msg_set, 1)
                    if isinstance(t, int) and t == -1:
                        act.wait_ge(sum_set, 1)
                        act.activation(conv_part(2, conv_hi), conv_part(2), ACT.Copy).then_inc(conv_rounded, 1)
                        act.wait_ge(gate_loaded, 16)
                        act.activation(gate_hi[:], gate, ACT.Copy).then_inc(gate_rounded, 1)
                if live(t, 1):
                    have(act, dist_done, a + 1)
                    have(act, att_set, a)
                    act.activation(expd[:], pF[:], ACT.Exp, scale=-1.0).then_inc(exp_set, 1)
                if live(t, -1):
                    have(act, hn2_set, d + 1)
                    have(act, uT_done, d)
                    act.activation(h2[:], hn2[:], ACT.Relu).then_inc(h2_set, 1)
                if live(t, -1):
                    have(act, uT_done, d + 1)
                    have(act, l1_done, d)
                    act.activation(uT[:], pH[:], ACT.Copy).then_inc(uT_set, 1)
                if live(t):
                    have(act, gates_done, g + 1)
                    act.activation(tr[:], pR[:], ACT.Tanh, bias=rz_b[:, 0:1], scale=0.5)
                    act.activation(ghn[:], pN[:], ACT.Identity, bias=hn_b[:, 0:1], scale=0.5).then_inc(ghn_set, 1)
                    have(act, oT_set, g)
                    act.activation(tz[:], pZ[:], ACT.Tanh, bias=rz_b[:, 1:2], scale=0.5).then_inc(tz_set, 1)
                if live(t, 1):
                    have(act, nmp_done, a + 1)
                    act.activation(n_hi[other][:], pF[:], ACT.Copy).then_inc(nhi_set, 1)
                if live(t):
                    have(act, v_set, g + 1)
                    act.activation(nn[:], v[:], ACT.Tanh, bias=vec[:, V_IN:V_IN + 1], scale=1.0).then_inc(nn_set, 1)

            steps(act, step)

        @block.vector
        def _(dve):
            def conv_low(n):
                dve.wait_ge(conv_rounded, n + 1)
                dve.tensor_tensor(conv_part(n, conv_lo), conv_part(n), conv_part(n, conv_hi).bitcast(F32),
                                  ALU.subtract).then_inc(conv_split, 1)

            def normalise1(t, u, par):
                b = t + 2
                loaded(dve, x_loaded, u, par, 2)
                for j in range(GG):
                    last = dve.bn_stats(st1[:, j, :], x_all[:, graph(b, j)])
                last.then_inc(st1_set, 1)
                have(dve, st1_set, b + 1)
                carry(dve)
                for j in range(GG):
                    last = dve.bn_aggr(mv1[:, j, :], st1[:, j, :])
                last.then_inc(mv1_set, 1)
                have(dve, mv1_set, b + 1)
                dve.tensor_scalar(ve1[:], mv1[:, :, 1], EPS, None, ALU.add).then_inc(ve1_set, 1)

            def apply1(t):
                b = t + 2
                have(dve, rs1_set, b + 1)
                have(dve, hT_placed, b)
                for j in range(GG):
                    last = dve.tensor_scalar(hn[:, j * N:(j + 1) * N], x_all[:, graph(b, j)], mv1[:, j, 0:1],
                                             rs1[:, j:j + 1], ALU.subtract, ALU.mult)
                last.then_inc(hn_set, 1)

            dve.memset(neg_half[:], -0.5).then_inc(half_set, 1)
            normalise1(-2, -1, 0)
            dve.wait_ge(vec_loaded, 16)
            dve.tensor_scalar(bn_var[:, 0:1], vec[:, V_V1:V_V1 + 1], EPS, None, ALU.add)
            dve.tensor_scalar(bn_var[:, 1:2], vec[:, V_V2:V_V2 + 1], EPS, None, ALU.add).then_inc(var_set, 1)
            dve.tensor_tensor(rz_s[:], vec[:, V_IR:V_IZ + 1], vec[:, V_HR:V_HZ + 1], ALU.add).then_inc(rzs_set, 1)
            dve.wait_ge(early_loaded, 16)
            dve.tensor_copy(early_hi[:], early[:, 0:2 * D]).then_inc(early_rounded, 1)
            dve.wait_ge(early_rounded, 1)
            dve.tensor_tensor(early_lo[:], early[:, 0:2 * D], early_hi[:].bitcast(F32), ALU.subtract)\
               .then_inc(early_split, 1)
            apply1(-2)
            dve.wait_ge(bnrs_set, 1)
            dve.tensor_tensor(bn_a[:, 0:1], bn_rs[:, 0:1], vec[:, V_G1:V_G1 + 1], ALU.mult)
            dve.tensor_tensor(bn_a[:, 1:2], bn_rs[:, 1:2], vec[:, V_G2:V_G2 + 1], ALU.mult).then_inc(bna_set, 1)
            dve.wait_ge(bna_set, 1)
            dve.tensor_tensor(bn_t[:, 0:1], bn_a[:, 0:1], vec[:, V_M1:V_M1 + 1], ALU.mult)
            dve.tensor_tensor(bn_t[:, 1:2], bn_a[:, 1:2], vec[:, V_M2:V_M2 + 1], ALU.mult).then_inc(bnt_set, 1)
            dve.wait_ge(bnt_set, 1)
            dve.tensor_tensor(bn_b[:, 0:1], vec[:, V_B1:V_B1 + 1], bn_t[:, 0:1], ALU.subtract)
            dve.tensor_tensor(bn_b[:, 1:2], vec[:, V_B2:V_B2 + 1], bn_t[:, 1:2], ALU.subtract)
            dve.wait_ge(rzs_set, 1)
            dve.tensor_scalar(rz_b[:], rz_s[:], 0.5, None, ALU.mult)
            dve.tensor_scalar(neg_a2[:], bn_a[:, 1:2], -1.0, None, ALU.mult)
            dve.tensor_scalar(hn_b[:], vec[:, V_HN:V_HN + 1], 0.5, None, ALU.mult).then_inc(vecs_set, 1)

            def step(t, u, par):
                a, g, d = t + 1, t, t - 1
                other = 1 - par
                if live(t, 1):
                    have(dve, hT_set, a + 1)
                    dve.tensor_copy(h_hi[other][:], hT[other][:]).then_inc(hhi_set, 1)
                    have(dve, hhi_set, a + 1)
                    dve.tensor_tensor(h_lo[other][:], hT[other][:], h_hi[other][:].bitcast(F32), ALU.subtract)\
                       .then_inc(hlo_set, 1)
                if isinstance(t, int) and t == -1:
                    conv_low(0)
                if live(t, 2):
                    normalise1(t, u, par)
                if live(t, 2):
                    apply1(t)
                if live(t, 1):
                    have(dve, sy_set, a + 1)
                    have(dve, dist_done, a)
                    dve.tensor_tensor(left[:], sx[0:SE, :], sy[0:SE, :], ALU.mult)
                    dve.tensor_tensor(right[:], sx[SE2:SE2 + SE, :], sy[SE2:SE2 + SE, :], ALU.mult).then_inc(lr_set, 1)
                if live(t, -1):
                    have(dve, o_placed, d + 1)
                    have(dve, x1b_set, d)
                    dve.scalar_tensor_tensor(x1[:], pH[:], 0.5, x_all[:, cols(d)], ALU.mult, ALU.add)\
                       .then_inc(x1_set, 1)
                if live(t, 1):
                    if isinstance(t, int) and t == -1:
                        dve.wait_ge(late_loaded, 16)
                    have(dve, msg_done, a + 1)
                    have(dve, msg_set, a)
                    dve.tensor_tensor(msg_t[:], pF[:], msg_bias, ALU.add).then_inc(msgt_set, 1)
                if isinstance(t, int) and t == -1:
                    conv_low(1)
                    dve.tensor_tensor(conv_part(2), conv[:, 0:TO * D], conv[:, TE * D:TAPS * D],
                                      ALU.add).then_inc(sum_set, 1)
                    conv_low(2)
                if live(t, -1):
                    have(dve, x1_set, d + 1)
                    for j in range(GG):
                        last = dve.bn_stats(st2[:, j, :], x1[:, j * N:(j + 1) * N])
                    last.then_inc(st2_set, 1)
                    have(dve, st2_set, d + 1)
                    carry(dve)
                    for j in range(GG):
                        last = dve.bn_aggr(mv2[:, j, :], st2[:, j, :])
                    last.then_inc(mv2_set, 1)
                    have(dve, mv2_set, d + 1)
                    dve.tensor_scalar(ve2[:], mv2[:, :, 1], EPS, None, ALU.add).then_inc(ve2_set, 1)
                if live(t):
                    phase = ct[:].rearrange("p (g m two) -> p g m two", g=GG, two=2)
                    pB = pBC[:, 0:W // 2].rearrange("p (g m) -> p g m", g=GG)
                    pC = pBC[:, W // 2:W].rearrange("p (g m) -> p g m", g=GG)
                    have(dve, conv2_done, g + 1)
                    have(dve, base_set, g + 1)
                    dve.scalar_tensor_tensor(odd[:], pC, bn_a[:, 1:2], base_o[:], ALU.mult, ALU.add)\
                       .then_inc(odd_set, 1)
                    dve.scalar_tensor_tensor(phase[:, :, :, 0], pB, bn_a[:, 1:2], base_e[:], ALU.mult, ALU.add)
                    have(dve, odd_set, g + 1)
                    dve.scalar_tensor_tensor(phase[:, :, :, 1], pB, neg_a2[:], odd[:], ALU.mult, ALU.add)\
                       .then_inc(ct_set, 1)
                    have(dve, ct_set, g + 1)
                    have(dve, gates_done, g)
                    dve.tensor_scalar(xc_hi[:], ct[:], 0.0, None, ALU.max).then_inc(xchi_set, 1)
                    have(dve, xchi_set, g + 1)
                    dve.scalar_tensor_tensor(xc_lo[:], ct[:], 0.0, xc_hi[:].bitcast(F32), ALU.max, ALU.subtract)\
                       .then_inc(xclo_set, 1)
                if live(t, -1):
                    have(dve, rs2_set, d + 1)
                    have(dve, h2_set, d)
                    for j in range(GG):
                        last = dve.tensor_scalar(hn2[:, j * N:(j + 1) * N], x1[:, j * N:(j + 1) * N],
                                                 mv2[:, j, 0:1], rs2[:, j:j + 1], ALU.subtract, ALU.mult)
                    last.then_inc(hn2_set, 1)
                if live(t, 1):
                    loaded(dve, adj_loaded, u, par, 1)
                    have(dve, exp_set, a + 1)
                    have(dve, nmp_done, a)
                    dve.tensor_tensor(attT[:], expd[:], adj_all[:, cols(a)], ALU.mult).then_inc(att_set, 1)
                if isinstance(t, int) and t == -1:
                    dve.wait_ge(gate_rounded, 1)
                    dve.tensor_tensor(gate_lo[:], gate, gate_hi[:].bitcast(F32), ALU.subtract).then_inc(gate_split, 1)
                if live(t):
                    have(dve, ghn_set, g + 1)
                    dve.scalar_tensor_tensor(rh[:], tr[:], 1.0, ghn[:], ALU.add, ALU.mult).then_inc(u_set, 1)
                    have(dve, u_set, g + 1)
                    dve.tensor_tensor(v[:], pI[:], rh[:], ALU.add).then_inc(v_set, 1)
                    have(dve, tz_set, g + 1)
                    dve.scalar_tensor_tensor(zh[:], tz[:], 1.0, hT[par][:], ALU.add, ALU.mult).then_inc(zh_set, 1)
                if live(t, 1):
                    have(dve, nhi_set, a + 1)
                    dve.tensor_tensor(n_lo[other][:], pF[:], n_hi[other][:].bitcast(F32), ALU.subtract)\
                       .then_inc(nlo_set, 1)
                if live(t):
                    have(dve, nn_set, g + 1)
                    dve.scalar_tensor_tensor(zn[:], tz[:], 1.0, nn[:], ALU.subtract, ALU.mult).then_inc(zn_set, 1)
                    have(dve, zn_set, g + 1)
                    have(dve, o_placed, g)
                    dve.tensor_tensor(oT[:], zh[:], zn[:], ALU.subtract).then_inc(oT_set, 1)
                if live(t, -1):
                    have(dve, l1_done, d + 1)
                    have(dve, x1b_set, d + 1)
                    dve.tensor_tensor(x_all[:, cols(d)], pH[:], x1b[:], ALU.add).then_inc(out_set, 1)

            steps(dve, step)

        @block.gpsimd
        def _(pool):
            pool.memset(ident[:], 0.0).then_inc(ident_zero, 1)
            pool.wait_ge(ident_zero, 1)
            pool.affine_select(out=ident[:], in_=ident[:], compare_op=ALU.not_equal, fill=1.0, base=0,
                               pattern=[[-1, 128]], channel_multiplier=1).then_inc(ident_set, 1)
            pool.memset(c1[:], 0.0).then_inc(pads_set, 1)
            pool.wait_ge(half_set, 1)
            pool.wait_ge(ve1_set, 1)
            pool.tensor_tensor(rs1[:], ve1[:], neg_half[:], ALU.pow).then_inc(rs1_set, 1)
            pool.wait_ge(var_set, 1)
            pool.tensor_tensor(bn_rs[:], bn_var[:], neg_half[:, 0:2], ALU.pow).then_inc(bnrs_set, 1)
            pool.wait_ge(vecs_set, 1)

            def step(t, u, par):
                a, g, d = t + 1, t, t - 1
                other = 1 - par
                if live(t):
                    have(pool, A2_set, g + 1)
                    have(pool, ct_set, g)
                    phase = hTb[par][:].rearrange("p (g m two) -> p g m two", g=GG, two=2)
                    pool.tensor_tensor(base_e[:], phase[:, :, :, 0], A2[:, :, 0:HALF], ALU.add)
                    pool.tensor_tensor(base_o[:], phase[:, :, :, 1], A2[:, :, 1:HALF + 1], ALU.subtract)\
                        .then_inc(base_set, 1)
                if live(t, 2):
                    have(pool, ve1_set, t + 3)
                    have(pool, hn_set, t + 2)
                    pool.tensor_tensor(rs1[:], ve1[:], neg_half[:], ALU.pow).then_inc(rs1_set, 1)
                if live(t, 1):
                    have(pool, hT_set, a + 1)
                    carry(pool)
                    pool.tensor_scalar(hTb[other][:], hT[other][:], bn_b[:, 1:2], 1.0, ALU.add, ALU.mult)\
                        .then_inc(hTb_set, 1)
                    have(pool, c1_set, a + 1)
                    pool.tensor_tensor(c1[:, 2, :, PE0:PO0 + HALF], c1[:, 0, :, PE0:PO0 + HALF],
                                       c1[:, 1, :, PE0:PO0 + HALF], ALU.add).then_inc(c1sum_set, 1)
                    have(pool, conv2_done, a - 1)
                    have(pool, c1sum_set, a + 1)
                    carry(pool)
                    pool.tensor_scalar(c1_hi[other][:], c1[:], 1.0, 0.0, ALU.mult, ALU.add).then_inc(c1hi_set, 1)
                    have(pool, c1hi_set, a + 1)
                    pool.tensor_tensor(c1_lo[other][:], c1[:], c1_hi[other][:].bitcast(F32), ALU.subtract)\
                        .then_inc(c1lo_set, 1)
                if live(t, -1):
                    have(pool, ve2_set, d + 1)
                    pool.tensor_tensor(rs2[:], ve2[:], neg_half[:], ALU.pow).then_inc(rs2_set, 1)
                    if isinstance(t, int) and t == 1:
                        pool.wait_ge(late_loaded, 16)
                    have(pool, out_set, d)
                    pool.tensor_tensor(x1b[:], x1[:], l1_bias, ALU.add).then_inc(x1b_set, 1)

            steps(pool, step)


def kernel(**inputs):
    import numpy as np
    import concourse.bacc as bacc
    from concourse.bass_utils import run_bass_kernel_spmd

    p = {k: np.asarray(v) for k, v in inputs.items()}
    f = {k.removeprefix("L0_gnn_"): v for k, v in p.items()}
    one, zero = np.ones(3, np.float32), np.zeros(3, np.float32)
    gap = np.zeros(SE2 - SE, np.float32)
    tail = np.zeros(128 - SE2 - SE, np.float32)
    b_se, w_se = f["b_se"], f["w_se"].T
    zw = np.zeros((D, 3), np.float32)
    se_x = np.concatenate([b_se, b_se, one, gap, b_se, one, b_se, tail])
    se_t = np.concatenate([one, b_se, one, gap, -2 * one, one, b_se, tail])
    se_a = np.concatenate([zero, one, zero, gap, zero, zero, one, tail])
    w_s = np.concatenate([w_se, w_se, zw, np.zeros((D, SE2 - SE), np.float32), w_se, zw, w_se,
                          np.zeros((D, 128 - SE2 - SE), np.float32)], axis=1)
    vec = np.stack([f["bn1_g"], f["bn1_b"], f["bn1_m"], f["bn1_v"], f["bn2_g"], f["bn2_b"], f["bn2_m"], f["bn2_v"],
                    *f["b_ih"].reshape(3, D), *f["b_hh"].reshape(3, D), se_x, se_t, se_a], axis=1)
    rows = lambda b: np.broadcast_to(np.tile(b, GG), (128, W))
    arrays = {
        "x_in": p["x"].transpose(1, 0, 2).reshape(N, B * D),
        "adj_in": p["adj"].transpose(2, 0, 1).reshape(N, B * N),
        "vec_in": vec,
        "early_in": np.concatenate([f["conv1_w"][:, :, 0].T, w_s, f["w_msg"].T], axis=1),
        "conv_in": np.concatenate([f["conv2_w"][:, :, 0::2], f["conv2_w"][:, :, 1::2]], axis=2)
        .transpose(1, 2, 0).reshape(D, TAPS * D),
        "gate_in": np.concatenate([f["w_ih"][:, 0:D].T, f["w_ih"][:, D:2 * D].T, f["w_hh"].T], axis=1),
        "late_in": np.concatenate([p["L1_gnn_weight"], rows(f["b_msg"]), rows(p["L1_gnn_bias"])], axis=1),
    }
    arrays = {k: np.ascontiguousarray(a) for k, a in arrays.items()}
    nc = bacc.Bacc("TRN2", target_bir_lowering=False, num_devices=1)
    args = [nc.dram_tensor(k, a.shape, F32, kind="ExternalInput").ap() for k, a in arrays.items()]
    out = nc.dram_tensor("out", (N, B * D), F32, kind="ExternalOutput").ap()
    gnn_kernel(nc, *args, out)
    r = run_bass_kernel_spmd(nc, [arrays], core_ids=[0])
    return r.results[0]["out"].reshape(N, B, D).transpose(1, 0, 2)
```

```python
import concourse.bass as bass
from concourse import mybir
from contextlib import ExitStack

F32 = mybir.dt.float32
F32R = mybir.dt.float32r
ALU = mybir.AluOpType
ACT = mybir.ActivationFunctionType
AX = mybir.AxisListType

B, N, D = 64, 128, 128
GG = 4
W = GG * N
NG = B // GG
TAPS = 17
PAD = TAPS // 2
EPS = 1e-5
S = 3
MS = D + S
SR = 4 * (S + 1)
V_G1, V_B1, V_M1, V_V1, V_G2, V_B2, V_M2, V_V2, V_IR, V_IZ, V_IN, V_HR, V_HZ, V_HN = range(14)
V_SB = 14
V_MASK = V_SB + GG * S
NV = V_MASK + GG
HALF = N // 2
TE, TO = (TAPS + 1) // 2, TAPS // 2
HA = HALF + 2
PW = HALF + TE + 2
PE0, PO0 = PAD // 2, PAD // 2 + 1


def gnn_kernel(nc, x_in, adj_in, vec_in, early_in, conv_in, gate_in, late_in, out):
    ctx = ExitStack()
    with ctx:
        def sb(name, shape, dt=F32):
            return ctx.enter_context(nc.sbuf_tensor(name, shape, dt))

        def pb(name):
            return ctx.enter_context(nc.psum_tensor(name, [128, 512], F32))

        def sem(name):
            return ctx.enter_context(nc.semaphore(name))

        x_all = sb("x_all", [128, B * D])
        adj_all = sb("adj_all", [128, B * N])
        vec = sb("vec", [128, NV])
        early = sb("early", [128, 2 * D + S])
        early_hi = sb("early_hi", [128, D], F32R)
        early_lo = sb("early_lo", [128, D], F32R)
        conv = x_all[:, B * D - (TAPS + TO) * D:]
        conv_hi = sb("conv_hi", [128, (TAPS + TO) * D], F32R)
        conv_lo = sb("conv_lo", [128, (TAPS + TO) * D], F32R)
        gate = x_all[:, B * D - (TAPS + TO + 9) * D:B * D - (TAPS + TO) * D]
        gate_hi = sb("gate_hi", [128, 9 * D], F32R)
        gate_lo = sb("gate_lo", [128, 9 * D], F32R)
        late = sb("late", [128, D + 2 * W])
        w_ms = early[:, D:MS + D]
        w_l1 = late[:, 0:D]
        msg_bias = late[:, D:D + W].rearrange("p (g d) -> p g d", g=GG)
        l1_bias = late[:, D + W:D + 2 * W]
        neg_half = sb("neg_half", [128, GG])
        warm = sb("warm", [128, 1])
        bn_var = sb("bn_var", [128, 2])
        bn_rs = sb("bn_rs", [128, 2])
        bn_a = sb("bn_a", [128, 2])
        bn_t = sb("bn_t", [128, 2])
        bn_b = sb("bn_b", [128, 2])
        rz_s = sb("rz_s", [128, 2])
        rz_b = sb("rz_b", [128, 2])
        hn_b = sb("hn_b", [128, 1])
        st1 = sb("st1", [128, GG, 6])
        mv1 = sb("mv1", [128, GG, 2])
        ve1 = sb("ve1", [128, GG])
        rs1 = sb("rs1", [128, GG])
        hn = sb("hn", [128, W])
        hT = [sb(f"hT{i}", [128, W]) for i in range(2)]
        hTb = [sb(f"hTb{i}", [128, W]) for i in range(2)]
        h_hi = [sb(f"h_hi{i}", [128, W], F32R) for i in range(2)]
        h_lo = [sb(f"h_lo{i}", [128, W], F32R) for i in range(2)]
        c1 = sb("c1", [128, 3, GG, PW])
        c1_hi = [sb(f"c1_hi{i}", [128, 3, GG, PW], F32R) for i in range(2)]
        c1_lo = [sb(f"c1_lo{i}", [128, 3, GG, PW], F32R) for i in range(2)]
        sq = sb("sq", [128, GG, S])
        sv = sb("sv", [128, GG, S + 1])
        svx = sb("svx", [128, GG, 2, S + 1], F32R)
        pair = sb("pair", [128, 2, GG, 2, 2, S + 1])
        left = sb("left", [GG * SR, N], F32R)
        right = sb("right", [GG * SR, GG, N], F32R)
        expd = sb("expd", [128, W])
        attT = sb("attT", [128, W])
        msg_t = sb("msg_t", [128, GG, D])
        msg = sb("msg", [128, W])
        n_hi = [sb(f"n_hi{i}", [128, W], F32R) for i in range(2)]
        n_lo = [sb(f"n_lo{i}", [128, W], F32R) for i in range(2)]
        A2 = sb("A2", [128, GG, HA])
        B2 = sb("B2", [128, GG, HALF])
        base_e = sb("base_e", [128, GG, HALF])
        base_o = sb("base_o", [128, GG, HALF])
        base_ob = sb("base_ob", [128, GG, HALF])
        ct = sb("ct", [128, W])
        xc_hi = sb("xc_hi", [128, W], F32R)
        xc_lo = sb("xc_lo", [128, W], F32R)
        tr = sb("tr", [128, W])
        tz = sb("tz", [128, W])
        ghn = sb("ghn", [128, W])
        rh = sb("rh", [128, W])
        v = sb("v", [128, W])
        nn = sb("nn", [128, W])
        zh = sb("zh", [128, W])
        zn = sb("zn", [128, W])
        oT = sb("oT", [128, W])
        x1 = sb("x1", [128, W])
        x1b = sb("x1b", [128, W])
        st2 = sb("st2", [128, GG, 6])
        mv2 = sb("mv2", [128, GG, 2])
        ve2 = sb("ve2", [128, GG])
        rs2 = sb("rs2", [128, GG])
        hn2 = sb("hn2", [128, W])
        h2 = sb("h2", [128, W])
        uT = sb("uT", [128, W])
        ident = sb("ident", [128, 128])

        pF = pb("pF")
        pH = pb("pH")
        pAC, pB = pb("pAC"), pb("pB")
        ms_front = pF[:, 0:(GG - 1) * MS].rearrange("p (g v) -> p g v", g=GG - 1)
        ms_last = pB[:, W // 2:W // 2 + MS]
        p_turn = pH[:, 0:N]
        pR, pZ, pI, pN = pb("pR"), pb("pZ"), pb("pI"), pb("pN")

        x_loaded = [sem(f"x_loaded{i}") for i in range(2)]
        adj_loaded = [sem(f"adj_loaded{i}") for i in range(2)]
        conv_loaded = [sem(f"conv_loaded_{i}") for i in ("even", "odd")]
        vec_loaded, early_loaded, gate_loaded, late_loaded = map(
            sem, ("vec_loaded", "early_loaded", "gate_loaded", "late_loaded"))
        stored = sem("stored")
        waits_carried = [sem(f"waits_carried_{e}") for e in ("dve", "pool")]
        half_set, var_set, bnrs_set, bna_set, bnt_set, bnb_set, rzs_set, vecs_set = map(
            sem, ("half_set", "var_set", "bnrs_set", "bna_set", "bnt_set", "bnb_set", "rzs_set", "vecs_set"))
        ident_zero, ident_set, pads_set = map(sem, ("ident_zero", "ident_set", "pads_set"))
        early_rounded, early_split, conv_rounded, conv_split, gate_rounded, gate_split = map(
            sem, ("early_rounded", "early_split", "conv_rounded", "conv_split", "gate_rounded", "gate_split"))
        sums_set, sums_rounded, sums_split, even0_rounded, even0_split = map(
            sem, ("sums_set", "sums_rounded", "sums_split", "even0_rounded", "even0_split"))
        st1_set, mv1_set, ve1_set, rs1_set, hn_set = map(sem, ("st1_set", "mv1_set", "ve1_set", "rs1_set", "hn_set"))
        hT_placed, hT_set, hhi_set, hlo_set, hTb_set = map(
            sem, ("hT_placed", "hT_set", "hhi_set", "hlo_set", "hTb_set"))
        conv1_done, c1_set, c1sum_set, c1hi_set, c1lo_set = map(
            sem, ("conv1_done", "c1_set", "c1sum_set", "c1hi_set", "c1lo_set"))
        s_set, sq_set, sv_set, svhi_set, svlo_set, ones_set, pair_set, turned, lr_set = map(
            sem, ("s_set", "sq_set", "sv_set", "svhi_set", "svlo_set", "ones_set", "pair_set", "turned",
                  "lr_set"))
        dist_done, exp_set, att_set = map(sem, ("dist_done", "exp_set", "att_set"))
        msg_done, msgt_set, msg_set = map(sem, ("msg_done", "msgt_set", "msg_set"))
        nmp_done, nhi_set, nlo_set = map(sem, ("nmp_done", "nhi_set", "nlo_set"))
        convA_done, A2_set, base_set, convB_done, B2_set, even_set, conv2_done, ct_set, xchi_set, xclo_set = map(
            sem, ("convA_done", "A2_set", "base_set", "convB_done", "B2_set", "even_set", "conv2_done", "ct_set", "xchi_set", "xclo_set"))
        hidden_done, gates_done = sem("hidden_done"), sem("gates_done")
        ghn_set, tr_set, tz_set, u_set, v_set, nn_set, zh_set, zn_set, oT_set = map(
            sem, ("ghn_set", "tr_set", "tz_set", "u_set", "v_set", "nn_set", "zh_set", "zn_set", "oT_set"))
        o_placed, x1_set, st2_set, mv2_set, ve2_set, rs2_set, hn2_set, h2_set, x1b_set = map(
            sem, ("o_placed", "x1_set", "st2_set", "mv2_set", "ve2_set", "rs2_set", "hn2_set", "h2_set", "x1b_set"))
        uT_done, uT_set, l1_done, out_set = map(sem, ("uT_done", "uT_set", "l1_done", "out_set"))

        def have(eng, s, n):
            if not isinstance(n, int) or n > 0:
                eng.wait_ge(s, n)

        def carry(eng):
            eng.sem_inc(waits_carried[eng is nc.gpsimd], 1)

        def steps(eng, step):
            for t in range(-1, 2):
                step(t, t // 2, t % 2)
            with eng.Fori(1, NG // 2 - 1) as u:
                step(2 * u, u, 0)
                step(2 * u + 1, u, 1)
            for t in range(NG - 2, NG + 1):
                step(t, t // 2, t % 2)

        def live(t, k=0):
            return not isinstance(t, int) or 0 <= t + k < NG

        def pieces(t, k=0):
            if isinstance(t, int) and t + k == NG - 1:
                return [(slice(0, W // 2), 0), (slice(W // 2, W), 1)]
            return [(slice(0, W), 0)]

        def back_bank(t, i):
            return (pAC, pB)[i] if len(pieces(t, -1)) > 1 else pH

        def graphs(c):
            return range(c.start // N, c.stop // N)

        def conv_part(n, whose=conv):
            return whose[:, (0, TE * D, TAPS * D)[n]:(TE * D, TAPS * D, (TAPS + TO) * D)[n]]

        def cols(g, c=slice(0, W)):
            return bass.ds(g * W + c.start, c.stop - c.start)

        def graph(g, j):
            return bass.ds(g * W + j * N, N)

        def loaded(eng, pair, u, par, k):
            eng.wait_ge(pair[(par + k) % 2], 16 * (u + (par + k) // 2 + 1))

        block = ctx.enter_context(nc.Block())

        @block.sync
        def _(sp):
            sp.dma_start(x_all[:, 0:W], x_in[:, 0:W]).then_inc(x_loaded[0], 16)
            sp.dma_start(early[:], early_in).then_inc(early_loaded, 16)
            sp.dma_start(x_all[:, W:2 * W], x_in[:, W:2 * W]).then_inc(x_loaded[1], 16)
            for n in range(2):
                c = slice((0, TE * D)[n], (TE * D, TAPS * D)[n])
                sp.dma_start(conv[:, c], conv_in[:, c]).then_inc(conv_loaded[n], 16)
            sp.dma_start(adj_all[:, 0:W], adj_in[:, 0:W]).then_inc(adj_loaded[0], 16)
            sp.dma_start(gate, gate_in).then_inc(gate_loaded, 16)
            sp.dma_start(adj_all[:, W:2 * W], adj_in[:, W:2 * W]).then_inc(adj_loaded[1], 16)

            def load(t, u, par):
                loaded(sp, x_loaded, u, par, 2)
                loaded(sp, adj_loaded, u, par, 2)
                sp.dma_start(x_all[:, cols(t + 4)], x_in[:, cols(t + 4)]).then_inc(x_loaded[par], 16)
                sp.dma_start(adj_all[:, cols(t + 4)], adj_in[:, cols(t + 4)]).then_inc(adj_loaded[par], 16)

            def step(t, u, par):
                if live(t, 4) and not (isinstance(t, int) and t + 4 < 2):
                    load(t, u, par)
                if live(t, -1):
                    for c, i in pieces(t, -1):
                        sp.wait_ge(out_set, t + i)
                        sp.dma_start(out[:, cols(t - 1, c)], x_all[:, cols(t - 1, c)]).then_inc(stored, 16)

            for t in range(-2, 2):
                step(t, t // 2, t % 2)
            sp.wait_ge(conv_split, 2)
            sp.wait_ge(gate_split, 1)
            with sp.Fori(1, NG // 2 - 2) as u:
                step(2 * u, u, 0)
                step(2 * u + 1, u, 1)
            for t in range(NG - 4, NG + 1):
                step(t, t // 2, t % 2)
            sp.wait_ge(stored, 16 * (NG + 1))

        @block.tensor
        def _(pe):
            def split_product(acc, w_hi, w_lo, m_hi, m_lo, start, stop):
                pe.matmul(acc, w_hi, m_hi, start=start, stop=False)
                pe.matmul(acc, w_hi, m_lo, start=False, stop=False)
                return pe.matmul(acc, w_lo, m_hi, start=False, stop=stop)

            def conv2_taps(par, product, lo, hi):
                taps = TO if product == 1 else TE
                acc = (pAC[:, 0:GG * HA], pB[:, 0:W // 2], pAC[:, 0:W // 2])[product]
                start, width = ((0, HA), (1, HALF), (1, HALF))[product]
                for k in range(lo, hi):
                    w = k if product == 0 or k == TO and product == 2 else (TE + k if product == 1 else TAPS + k)
                    last = split_product(acc, conv_hi[:, w * D:(w + 1) * D], conv_lo[:, w * D:(w + 1) * D],
                                         c1_hi[par][:, product, :, start + k:start + k + width],
                                         c1_lo[par][:, product, :, start + k:start + k + width],
                                         start=k == 0, stop=k == taps - 1)
                return last

            def gate_part(acc, part, which, m_hi, m_lo, start, stop):
                w = slice((3 * part + which) * D, (3 * part + which + 1) * D)
                return split_product(acc[:], gate_hi[:, w], gate_lo[:, w], m_hi[:], m_lo[:], start, stop)

            def step(t, u, par):
                a, g, d = t + 1, t, t - 1
                other = 1 - par
                def conv_a():
                    if t_is(0):
                        pe.wait_ge(conv_split, 1)
                        pe.wait_ge(even0_split, 1)
                    else:
                        have(pe, c1lo_set, g + 1)
                    have(pe, ct_set, g)
                    conv2_taps(par, 0, 0, TE).then_inc(convA_done, 1)

                def conv_b():
                    if t_is(0):
                        pe.wait_ge(conv_split, 2)
                        pe.wait_ge(c1lo_set, 1)
                    have(pe, msgt_set, g + 1)
                    conv2_taps(par, 1, 0, TO).then_inc(convB_done, 1)

                def conv_c1():
                    if t_is(0):
                        pe.wait_ge(sums_split, 1)
                    have(pe, A2_set, g + 1)
                    conv2_taps(par, 2, 0, 4)

                def conv_c2():
                    conv2_taps(par, 2, 4, TE).then_inc(conv2_done, 1)

                def x_turn(q):
                    have(pe, hn_set, q + 1)
                    have(pe, nlo_set, q)
                    for j in range(GG):
                        last = pe.transpose(pF[:, j * N:(j + 1) * N], hn[:, j * N:(j + 1) * N], ident[:])
                    last.then_inc(hT_placed, 1)

                def conv1_messages(q, p):
                    if t_is(-1):
                        pe.wait_ge(early_split, 1)
                    have(pe, hlo_set, q + 1)
                    have(pe, x1_set, q - 1)
                    split_product(pH[:], early_hi[:], early_lo[:], h_hi[p][:], h_lo[p][:],
                                  True, True).then_inc(conv1_done, 1)
                    for j in range(GG):
                        if j == GG - 1:
                            have(pe, B2_set, q)
                        last = pe.matmul(ms_last if j == GG - 1 else ms_front[:, j, :],
                                         hT[p][:, j * N:(j + 1) * N], w_ms, start=True, stop=True)
                    last.then_inc(msg_done, 1)

                def rows_turn(q):
                    have(pe, pair_set, q + 1)
                    have(pe, c1_set, q + 1)
                    pe.transpose(p_turn, pair[:].rearrange("p s g x y v -> p (s g x y v)"), ident[:])\
                      .then_inc(turned, 1)

                def distances(q):
                    have(pe, lr_set, q + 1)
                    have(pe, msgt_set, q + 1)
                    pe.matmul(pF[:], left[:], right[:].rearrange("r g n -> r (g n)"), start=True, stop=True)\
                      .then_inc(dist_done, 1)

                def neighbour_sums(q):
                    have(pe, att_set, q + 1)
                    have(pe, msg_set, q + 1)
                    for j in range(GG):
                        last = pe.matmul(pF[:, j * N:(j + 1) * N], msg[:, j * N:(j + 1) * N],
                                         attT[:, j * N:(j + 1) * N], start=True, stop=True)
                    last.then_inc(nmp_done, 1)

                def gates_h():
                    if t_is(0):
                        pe.wait_ge(gate_split, 1)
                    have(pe, v_set, g)
                    have(pe, tz_set, g)
                    gate_part(pN, 2, 2, h_hi[par], h_lo[par], True, True).then_inc(hidden_done, 1)
                    gate_part(pR, 2, 0, h_hi[par], h_lo[par], True, False)
                    gate_part(pZ, 2, 1, h_hi[par], h_lo[par], True, False)

                def gates_n():
                    have(pe, nlo_set, g + 1)
                    gate_part(pR, 1, 0, n_hi[par], n_lo[par], False, False)
                    gate_part(pZ, 1, 1, n_hi[par], n_lo[par], False, False)
                    gate_part(pI, 1, 2, n_hi[par], n_lo[par], True, False)

                def gates_c():
                    have(pe, xclo_set, g + 1)
                    gate_part(pR, 0, 0, xc_hi, xc_lo, False, True).then_inc(gates_done, 1)
                    gate_part(pZ, 0, 1, xc_hi, xc_lo, False, True).then_inc(gates_done, 1)
                    gate_part(pI, 0, 2, xc_hi, xc_lo, False, True).then_inc(gates_done, 1)

                def o_turn():
                    if live(t):
                        have(pe, out_set, d)
                    for c, i in pieces(t, -1):
                        have(pe, oT_set, d + 1 + i)
                        for j in graphs(c):
                            last = pe.transpose(back_bank(t, i)[:, j * N:(j + 1) * N], oT[:, j * N:(j + 1) * N], ident[:])
                        last.then_inc(o_placed, 1)

                def adj_h2():
                    for c, i in pieces(t, -1):
                        have(pe, h2_set, d + 1 + i)
                        for j in graphs(c):
                            last = pe.matmul(back_bank(t, i)[:, j * N:(j + 1) * N], h2[:, j * N:(j + 1) * N],
                                             adj_all[:, graph(d, j)], start=True, stop=True)
                        last.then_inc(uT_done, 1)

                def layer2():
                    if t_is(1):
                        pe.wait_ge(late_loaded, 16)
                    for c, i in pieces(t, -1):
                        have(pe, uT_set, d + 1 + i)
                        for j in graphs(c):
                            last = pe.matmul(back_bank(t, i)[:, j * N:(j + 1) * N], uT[:, j * N:(j + 1) * N], w_l1,
                                             start=True, stop=True)
                        last.then_inc(l1_done, 1)

                def keep_clock(n):
                    for _ in range(n):
                        pe.matmul(pAC[:, 0:N], ident[:], ident[:], start=True, stop=True)

                def t_is(n):
                    return isinstance(t, int) and t == n

                front, middle, back = live(t, 1), live(t), live(t, -1)
                if t_is(-1):
                    pe.wait_ge(ident_set, 1)
                    keep_clock(17)
                    x_turn(a)
                    keep_clock(9)
                    conv1_messages(a, other)
                    keep_clock(4)
                    return
                if t_is(0):
                    conv_a()
                    rows_turn(g)
                    conv_b()
                    distances(g)
                    conv_c1()
                    neighbour_sums(g)
                    conv_c2()
                    x_turn(a)
                    gates_h()
                    conv1_messages(a, other)
                    gates_n()
                    rows_turn(a)
                    gates_c()
                    distances(a)
                    neighbour_sums(a)
                    return
                if middle:
                    conv_a()
                if back:
                    o_turn()
                if front:
                    x_turn(a)
                if middle:
                    conv_b()
                if front:
                    conv1_messages(a, other)
                if middle:
                    conv_c1()
                    conv_c2()
                if front:
                    rows_turn(a)
                if middle:
                    gates_h()
                if front:
                    distances(a)
                if middle:
                    gates_n()
                if back:
                    adj_h2()
                if middle:
                    gates_c()
                if back:
                    layer2()
                if front:
                    neighbour_sums(a)

            steps(pe, step)

        @block.scalar
        def _(act):
            act.dma_start(vec[:], vec_in).then_inc(vec_loaded, 16)
            act.dma_start(late[:], late_in).then_inc(late_loaded, 16)
            act.wait_ge(half_set, 1)
            act.activation(warm[:], neg_half[:, 0:1], ACT.Tanh)
            act.wait_ge(conv_loaded[0], 16)
            act.activation(conv_part(0, conv_hi), conv_part(0), ACT.Copy).then_inc(conv_rounded, 1)

            def scale_a(g):
                have(act, convA_done, g + 1)
                have(act, base_set, g)
                act.activation(A2[:].rearrange("p g m -> p (g m)"), pAC[:, 0:GG * HA], ACT.Identity, bias=0.0,
                               scale=bn_a[:, 1:2]).then_inc(A2_set, 1)

            def scale_b(g):
                have(act, convB_done, g + 1)
                have(act, even_set, g)
                act.activation(B2[:].rearrange("p g m -> p (g m)"), pB[:, 0:W // 2], ACT.Identity, bias=0.0,
                               scale=bn_a[:, 1:2]).then_inc(B2_set, 1)

            def step(t, u, par):
                a, g, d = t + 1, t, t - 1
                other = 1 - par
                if live(t) and not (isinstance(t, int) and t == 0):
                    scale_a(g)
                if live(t, 1):
                    have(act, hT_placed, a + 1)
                    have(act, zh_set, a - 1)
                    act.activation(hT[other][:], pF[:], ACT.Relu).then_inc(hT_set, 1)
                if live(t) and not (isinstance(t, int) and t == 0):
                    scale_b(g)
                if live(t, 1):
                    if isinstance(t, int) and t == -1:
                        act.wait_ge(conv_loaded[1], 16)
                        act.activation(conv_part(1, conv_hi), conv_part(1), ACT.Copy).then_inc(conv_rounded, 1)
                        act.wait_ge(pads_set, 1)
                        act.wait_ge(vecs_set, 1)
                    have(act, conv1_done, a + 1)
                    have(act, c1lo_set, a)
                    if isinstance(t, int) and t == 0:
                        act.wait_ge(even0_split, 1)
                    nodes = pH[:].rearrange("p (g m two) -> p g m two", g=GG, two=2)
                    act.activation(c1[:, 0, :, PE0:PE0 + HALF], nodes[:, :, :, 0], ACT.Relu, bias=bn_b[:, 0:1],
                                   scale=bn_a[:, 0:1])
                    act.activation(c1[:, 1, :, PO0:PO0 + HALF], nodes[:, :, :, 1], ACT.Relu, bias=bn_b[:, 0:1],
                                   scale=bn_a[:, 0:1]).then_inc(c1_set, 1)
                    if isinstance(t, int) and t == -1:
                        act.wait_ge(gate_loaded, 16)
                        act.activation(gate_hi[:], gate, ACT.Copy).then_inc(gate_rounded, 1)
                    have(act, msgt_set, a + 1)
                    have(act, nmp_done, a)
                    act.activation(msg[:], msg_t[:].rearrange("p g d -> p (g d)"), ACT.Relu).then_inc(msg_set, 1)
                if live(t, -1):
                    have(act, uT_done, d)
                    for c, i in pieces(t, -1):
                        have(act, hn2_set, d + 1 + i)
                        act.activation(h2[:, c], hn2[:, c], ACT.Relu).then_inc(h2_set, 1)
                if isinstance(t, int) and t == -1:
                    scale_a(0)
                    scale_b(0)
                if live(t, 1):
                    have(act, dist_done, a + 1)
                    have(act, att_set, a)
                    act.activation(expd[:], pF[:], ACT.Exp, scale=-1.0).then_inc(exp_set, 1)
                if live(t):
                    have(act, hidden_done, g + 1)
                    act.activation(ghn[:], pN[:], ACT.Identity, bias=hn_b[:, 0:1], scale=0.5).then_inc(ghn_set, 1)
                if live(t, -1):
                    have(act, l1_done, d)
                    for c, i in pieces(t, -1):
                        have(act, uT_done, d + 1 + i)
                        act.activation(uT[:, c], back_bank(t, i)[:, c], ACT.Copy).then_inc(uT_set, 1)
                if live(t):
                    have(act, gates_done, 3 * g + 1)
                    act.activation(tr[:], pR[:], ACT.Tanh, bias=rz_b[:, 0:1], scale=0.5).then_inc(tr_set, 1)
                    have(act, gates_done, 3 * g + 2)
                    have(act, oT_set, g)
                    act.activation(tz[:], pZ[:], ACT.Tanh, bias=rz_b[:, 1:2], scale=0.5).then_inc(tz_set, 1)
                if live(t, 1):
                    have(act, nmp_done, a + 1)
                    act.activation(n_hi[other][:], pF[:], ACT.Copy).then_inc(nhi_set, 1)
                if live(t):
                    for c, i in pieces(t):
                        have(act, v_set, g + 1 + i)
                        act.activation(nn[:, c], v[:, c], ACT.Tanh, bias=vec[:, V_IN:V_IN + 1], scale=1.0)\
                           .then_inc(nn_set, 1)

            steps(act, step)

        @block.vector
        def _(dve):
            def conv_low(n):
                dve.wait_ge(conv_rounded, n + 1)
                dve.tensor_tensor(conv_part(n, conv_lo), conv_part(n), conv_part(n, conv_hi).bitcast(F32),
                                  ALU.subtract).then_inc(conv_split, 1)

            def normalise1(t, u, par):
                b = t + 2
                loaded(dve, x_loaded, u, par, 2)
                for j in range(GG):
                    last = dve.bn_stats(st1[:, j, :], x_all[:, graph(b, j)])
                last.then_inc(st1_set, 1)
                have(dve, st1_set, b + 1)
                carry(dve)
                for j in range(GG):
                    last = dve.bn_aggr(mv1[:, j, :], st1[:, j, :])
                last.then_inc(mv1_set, 1)
                have(dve, mv1_set, b + 1)
                dve.tensor_scalar(ve1[:], mv1[:, :, 1], EPS, None, ALU.add).then_inc(ve1_set, 1)

            def apply1(t):
                b = t + 2
                have(dve, rs1_set, b + 1)
                have(dve, hT_placed, b)
                for j in range(GG):
                    last = dve.tensor_scalar(hn[:, j * N:(j + 1) * N], x_all[:, graph(b, j)], mv1[:, j, 0:1],
                                             rs1[:, j:j + 1], ALU.subtract, ALU.mult)
                last.then_inc(hn_set, 1)

            def moments2(c, n):
                have(dve, x1_set, n)
                for j in graphs(c):
                    last = dve.bn_stats(st2[:, j, :], x1[:, j * N:(j + 1) * N])
                last.then_inc(st2_set, 1)
                have(dve, st2_set, n)
                carry(dve)
                for j in graphs(c):
                    last = dve.bn_aggr(mv2[:, j, :], st2[:, j, :])
                last.then_inc(mv2_set, 1)
                have(dve, mv2_set, n)
                j = slice(c.start // N, c.stop // N)
                dve.tensor_scalar(ve2[:, j], mv2[:, j, 1], EPS, None, ALU.add).then_inc(ve2_set, 1)

            dve.memset(neg_half[:], -0.5).then_inc(half_set, 1)
            normalise1(-2, -1, 0)
            dve.wait_ge(vec_loaded, 16)
            dve.tensor_scalar(bn_var[:, 0:1], vec[:, V_V1:V_V1 + 1], EPS, None, ALU.add)
            dve.tensor_scalar(bn_var[:, 1:2], vec[:, V_V2:V_V2 + 1], EPS, None, ALU.add).then_inc(var_set, 1)
            dve.tensor_tensor(rz_s[:], vec[:, V_IR:V_IZ + 1], vec[:, V_HR:V_HZ + 1], ALU.add).then_inc(rzs_set, 1)
            dve.wait_ge(early_loaded, 16)
            dve.tensor_copy(early_hi[:], early[:, 0:D]).then_inc(early_rounded, 1)
            dve.wait_ge(early_rounded, 1)
            dve.tensor_tensor(early_lo[:], early[:, 0:D], early_hi[:].bitcast(F32), ALU.subtract)\
               .then_inc(early_split, 1)
            apply1(-2)
            dve.wait_ge(bnrs_set, 1)
            dve.tensor_tensor(bn_a[:, 0:1], bn_rs[:, 0:1], vec[:, V_G1:V_G1 + 1], ALU.mult)
            dve.tensor_tensor(bn_a[:, 1:2], bn_rs[:, 1:2], vec[:, V_G2:V_G2 + 1], ALU.mult).then_inc(bna_set, 1)
            dve.wait_ge(bna_set, 1)
            dve.tensor_tensor(bn_t[:, 0:1], bn_a[:, 0:1], vec[:, V_M1:V_M1 + 1], ALU.mult)
            dve.tensor_tensor(bn_t[:, 1:2], bn_a[:, 1:2], vec[:, V_M2:V_M2 + 1], ALU.mult).then_inc(bnt_set, 1)
            dve.wait_ge(bnt_set, 1)
            dve.tensor_tensor(bn_b[:, 0:1], vec[:, V_B1:V_B1 + 1], bn_t[:, 0:1], ALU.subtract)
            dve.tensor_tensor(bn_b[:, 1:2], vec[:, V_B2:V_B2 + 1], bn_t[:, 1:2], ALU.subtract)
            dve.wait_ge(rzs_set, 1)
            dve.tensor_scalar(rz_b[:], rz_s[:], 0.5, None, ALU.mult)
            dve.tensor_scalar(hn_b[:], vec[:, V_HN:V_HN + 1], 0.5, None, ALU.mult).then_inc(vecs_set, 1)
            normalise1(-1, -1, 1)

            def step(t, u, par):
                a, g, d = t + 1, t, t - 1
                other, first = 1 - par, isinstance(t, int) and t == -1
                if live(t, -1):
                    have(dve, x1b_set, d)
                    for c, i in pieces(t, -1):
                        have(dve, o_placed, d + 1 + i)
                        dve.scalar_tensor_tensor(x1[:, c], back_bank(t, i)[:, c], 0.5, x_all[:, cols(d, c)], ALU.mult, ALU.add)\
                           .then_inc(x1_set, 1)
                        if not live(t, 1):
                            moments2(c, d + 1 + i)
                if live(t, 1):
                    have(dve, hT_set, a + 1)
                    dve.tensor_copy(h_hi[other][:], hT[other][:]).then_inc(hhi_set, 1)
                    have(dve, hhi_set, a + 1)
                    dve.tensor_tensor(h_lo[other][:], hT[other][:], h_hi[other][:].bitcast(F32), ALU.subtract)\
                       .then_inc(hlo_set, 1)
                if live(t, 1) and live(t, -1):
                    moments2(slice(0, W), d + 1)
                if live(t, 2) and not first:
                    normalise1(t, u, par)
                if first:
                    conv_low(0)
                    dve.wait_ge(c1_set, 1)
                    dve.tensor_copy(c1_hi[0][:, 0], c1[:, 0]).then_inc(even0_rounded, 1)
                    dve.wait_ge(even0_rounded, 1)
                    dve.tensor_tensor(c1_lo[0][:, 0], c1[:, 0], c1_hi[0][:, 0].bitcast(F32), ALU.subtract)\
                       .then_inc(even0_split, 1)
                if live(t, 1):
                    if first:
                        dve.wait_ge(ones_set, 1)
                    bias = vec[:, V_SB:V_SB + GG * S].rearrange("p (g v) -> p g v", g=GG)
                    halves = svx[:].bitcast(F32)
                    rows = pair[:].rearrange("p s g x y v -> p s (g x) y v")
                    have(dve, msg_done, a + 1)
                    dve.tensor_tensor(sv[:, 0:GG - 1, 0:S], ms_front[:, :, D:MS], bias[:, 0:GG - 1, :], ALU.add)
                    dve.tensor_tensor(sv[:, GG - 1, 0:S], ms_last[:, D:MS], bias[:, GG - 1, :], ALU.add)\
                       .then_inc(s_set, 1)
                    have(dve, s_set, a + 1)
                    dve.tensor_tensor(sq[:], sv[:, :, 0:S], sv[:, :, 0:S], ALU.mult).then_inc(sq_set, 1)
                    have(dve, sq_set, a + 1)
                    dve.tensor_reduce(sv[:, :, S], sq[:], AX.X, ALU.add).then_inc(sv_set, 1)
                    have(dve, sv_set, a + 1)
                    dve.tensor_copy(svx[:, :, 0, :], sv[:]).then_inc(svhi_set, 1)
                    have(dve, svhi_set, a + 1)
                    dve.tensor_tensor(svx[:, :, 1, :], sv[:], halves[:, :, 0, :], ALU.subtract).then_inc(svlo_set, 1)
                    have(dve, svlo_set, a + 1)
                    have(dve, turned, a)
                    of_x = halves.rearrange("p g x v -> p (g x) v")
                    dve.tensor_copy(rows[:, 0, :, 0, 0:S], of_x[:, :, 0:S])
                    dve.tensor_copy(rows[:, 0, :, 1, 0:S], of_x[:, :, 0:S])
                    for x in range(2):
                        dve.tensor_scalar(pair[:, 1, :, x, :, 0:S], halves[:, :, :, 0:S], -2.0, None, ALU.mult)
                    dve.tensor_copy(rows[:, 0, :, 0, S], of_x[:, :, S])
                    dve.tensor_copy(rows[:, 1, :, 1, S], of_x[:, :, S]).then_inc(pair_set, 1)
                if live(t, 1):
                    if first:
                        dve.wait_ge(late_loaded, 16)
                    have(dve, msg_set, a)
                    dve.tensor_tensor(msg_t[:, 0:GG - 1, :], ms_front[:, :, 0:D], msg_bias[:, 0:GG - 1, :], ALU.add)
                    dve.tensor_tensor(msg_t[:, GG - 1, :], ms_last[:, 0:D], msg_bias[:, GG - 1, :], ALU.add)\
                       .then_inc(msgt_set, 1)
                if first:
                    conv_low(1)
                if live(t, 1):
                    have(dve, turned, a + 1)
                    have(dve, dist_done, a)
                    dve.tensor_copy(left[:], p_turn[0:GG * SR, :])
                    dve.tensor_tensor(right[:], p_turn[GG * SR:2 * GG * SR, :].unsqueeze(1)
                                      .to_broadcast([GG * SR, GG, N]),
                                      vec[GG * SR:2 * GG * SR, V_MASK:V_MASK + GG].unsqueeze(2)
                                      .to_broadcast([GG * SR, GG, N]), ALU.mult).then_inc(lr_set, 1)
                if first:
                    apply1(t)
                if live(t, -1):
                    have(dve, h2_set, d)
                    for c, i in pieces(t, -1):
                        have(dve, rs2_set, d + 1 + i)
                        for j in graphs(c):
                            last = dve.tensor_scalar(hn2[:, j * N:(j + 1) * N], x1[:, j * N:(j + 1) * N],
                                                     mv2[:, j, 0:1], rs2[:, j:j + 1], ALU.subtract, ALU.mult)
                        last.then_inc(hn2_set, 1)
                if live(t):
                    phase = ct[:].rearrange("p (g m two) -> p g m two", g=GG, two=2)
                    have(dve, conv2_done, g + 1)
                    have(dve, even_set, g + 1)
                    dve.scalar_tensor_tensor(phase[:, :, :, 1], pAC[:, 0:W // 2].rearrange("p (g m) -> p g m", g=GG),
                                             bn_a[:, 1:2], base_ob[:], ALU.mult, ALU.add).then_inc(ct_set, 1)
                    have(dve, ct_set, g + 1)
                    have(dve, gates_done, 3 * g)
                    dve.tensor_scalar(xc_hi[:], ct[:], 0.0, None, ALU.max).then_inc(xchi_set, 1)
                    have(dve, xchi_set, g + 1)
                    dve.scalar_tensor_tensor(xc_lo[:], ct[:], 0.0, xc_hi[:].bitcast(F32), ALU.max, ALU.subtract)\
                       .then_inc(xclo_set, 1)
                if live(t, 1):
                    loaded(dve, adj_loaded, u, par, 1)
                    have(dve, exp_set, a + 1)
                    have(dve, nmp_done, a)
                    dve.tensor_tensor(attT[:], expd[:], adj_all[:, cols(a)], ALU.mult).then_inc(att_set, 1)
                if live(t, 2) and not first:
                    apply1(t)
                if live(t):
                    have(dve, ghn_set, g + 1)
                    have(dve, tr_set, g + 1)
                    dve.scalar_tensor_tensor(rh[:], tr[:], 1.0, ghn[:], ALU.add, ALU.mult).then_inc(u_set, 1)
                    have(dve, u_set, g + 1)
                    have(dve, gates_done, 3 * g + 3)
                    for c, i in pieces(t):
                        dve.tensor_tensor(v[:, c], pI[:, c], rh[:, c], ALU.add).then_inc(v_set, 1)
                    have(dve, tz_set, g + 1)
                    dve.scalar_tensor_tensor(zh[:], tz[:], 1.0, hT[par][:], ALU.add, ALU.mult).then_inc(zh_set, 1)
                if live(t, -1):
                    have(dve, x1b_set, d + 1)
                    for c, i in pieces(t, -1):
                        have(dve, l1_done, d + 1 + i)
                        dve.tensor_tensor(x_all[:, cols(d, c)], back_bank(t, i)[:, c], x1b[:, c], ALU.add)\
                           .then_inc(out_set, 1)
                if live(t, 1):
                    have(dve, nhi_set, a + 1)
                    dve.tensor_tensor(n_lo[other][:], pF[:], n_hi[other][:].bitcast(F32), ALU.subtract)\
                       .then_inc(nlo_set, 1)
                if live(t):
                    have(dve, o_placed, g)
                    for c, i in pieces(t):
                        have(dve, nn_set, g + 1 + i)
                        dve.scalar_tensor_tensor(zn[:, c], tz[:, c], 1.0, nn[:, c], ALU.subtract, ALU.mult)\
                           .then_inc(zn_set, 1)
                        have(dve, zn_set, g + 1 + i)
                        dve.tensor_tensor(oT[:, c], zh[:, c], zn[:, c], ALU.subtract).then_inc(oT_set, 1)

            steps(dve, step)

        @block.gpsimd
        def _(pool):
            pool.memset(ident[:], 0.0).then_inc(ident_zero, 1)
            pool.wait_ge(ident_zero, 1)
            pool.affine_select(out=ident[:], in_=ident[:], compare_op=ALU.not_equal, fill=1.0, base=0,
                               pattern=[[-1, 128]], channel_multiplier=1).then_inc(ident_set, 1)
            pool.memset(c1[:], 0.0).then_inc(pads_set, 1)
            pool.memset(pair[:, 0, :, :, 1, S:S + 1], 1.0)
            pool.memset(pair[:, 1, :, :, 0, S:S + 1], 1.0).then_inc(ones_set, 1)
            pool.wait_ge(half_set, 1)
            pool.wait_ge(ve1_set, 1)
            pool.tensor_tensor(rs1[:], ve1[:], neg_half[:], ALU.pow).then_inc(rs1_set, 1)
            pool.wait_ge(var_set, 1)
            pool.tensor_tensor(bn_rs[:], bn_var[:], neg_half[:, 0:2], ALU.pow).then_inc(bnrs_set, 1)
            for n in range(2):
                pool.wait_ge(conv_loaded[n], 16)
            pool.tensor_tensor(conv_part(2), conv[:, 0:TO * D], conv[:, TE * D:TAPS * D], ALU.add).then_inc(sums_set, 1)
            pool.wait_ge(sums_set, 1)
            pool.tensor_scalar(conv_part(2, conv_hi), conv_part(2), 1.0, 0.0, ALU.mult, ALU.add)\
                .then_inc(sums_rounded, 1)
            pool.wait_ge(sums_rounded, 1)
            pool.tensor_tensor(conv_part(2, conv_lo), conv_part(2), conv_part(2, conv_hi).bitcast(F32),
                               ALU.subtract).then_inc(sums_split, 1)
            pool.wait_ge(vecs_set, 1)

            def shift_h(t, par):
                carry(pool)
                pool.tensor_scalar(hTb[1 - par][:], hT[1 - par][:], bn_b[:, 1:2], 1.0, ALU.add, ALU.mult)\
                    .then_inc(hTb_set, 1)

            def step(t, u, par):
                a, g, d = t + 1, t, t - 1
                other = 1 - par
                if live(t):
                    have(pool, hTb_set, g + 1)
                    have(pool, A2_set, g + 1)
                    have(pool, ct_set, g)
                    phase = hTb[par][:].rearrange("p (g m two) -> p g m two", g=GG, two=2)
                    pool.tensor_tensor(base_e[:], phase[:, :, :, 0], A2[:, :, 0:HALF], ALU.add)
                    pool.tensor_tensor(base_o[:], phase[:, :, :, 1], A2[:, :, 1:HALF + 1], ALU.subtract)\
                        .then_inc(base_set, 1)
                    have(pool, base_set, g + 1)
                    have(pool, B2_set, g + 1)
                    have(pool, xclo_set, g)
                    evens = ct[:].rearrange("p (g m two) -> p g m two", g=GG, two=2)[:, :, :, 0]
                    pool.tensor_tensor(evens, base_e[:], B2[:], ALU.add)
                    pool.tensor_tensor(base_ob[:], base_o[:], B2[:], ALU.subtract).then_inc(even_set, 1)
                if live(t, -1):
                    for c, i in pieces(t, -1):
                        have(pool, ve2_set, d + 1 + i)
                        j = slice(c.start // N, c.stop // N)
                        pool.tensor_tensor(rs2[:, j], ve2[:, j], neg_half[:, j], ALU.pow).then_inc(rs2_set, 1)
                if live(t, 1):
                    first = isinstance(t, int) and t == -1
                    phases = slice(1 if first else 0, 3)
                    have(pool, hT_set, a + 1)
                    if not first:
                        shift_h(t, par)
                    have(pool, c1_set, a + 1)
                    pool.tensor_tensor(c1[:, 2, :, PE0:PO0 + HALF], c1[:, 0, :, PE0:PO0 + HALF],
                                       c1[:, 1, :, PE0:PO0 + HALF], ALU.add).then_inc(c1sum_set, 1)
                    have(pool, conv2_done, a - 1)
                    have(pool, c1sum_set, a + 1)
                    carry(pool)
                    pool.tensor_scalar(c1_hi[other][:, phases], c1[:, phases], 1.0, 0.0, ALU.mult, ALU.add)\
                        .then_inc(c1hi_set, 1)
                    have(pool, c1hi_set, a + 1)
                    pool.tensor_tensor(c1_lo[other][:, phases], c1[:, phases], c1_hi[other][:, phases].bitcast(F32),
                                       ALU.subtract).then_inc(c1lo_set, 1)
                if live(t, 2):
                    have(pool, ve1_set, t + 3)
                    have(pool, hn_set, t + 2)
                    pool.tensor_tensor(rs1[:], ve1[:], neg_half[:], ALU.pow).then_inc(rs1_set, 1)
                if isinstance(t, int) and t == -1:
                    shift_h(t, par)
                    pool.wait_ge(gate_rounded, 1)
                    pool.tensor_tensor(gate_lo[:], gate, gate_hi[:].bitcast(F32), ALU.subtract).then_inc(gate_split, 1)
                if live(t, -1):
                    if isinstance(t, int) and t == 1:
                        pool.wait_ge(late_loaded, 16)
                    have(pool, out_set, d)
                    pool.tensor_tensor(x1b[:], x1[:], l1_bias, ALU.add).then_inc(x1b_set, 1)

            steps(pool, step)


def kernel(**inputs):
    import numpy as np
    import concourse.bacc as bacc
    from concourse.bass_utils import run_bass_kernel_spmd

    p = {k: np.asarray(v) for k, v in inputs.items()}
    f = {k.removeprefix("L0_gnn_"): v for k, v in p.items()}
    mask = np.concatenate([np.zeros((GG * SR, GG), np.float32), np.repeat(np.eye(GG, dtype=np.float32), SR, axis=0)])
    vec = np.stack([f["bn1_g"], f["bn1_b"], f["bn1_m"], f["bn1_v"], f["bn2_g"], f["bn2_b"], f["bn2_m"], f["bn2_v"],
                    *f["b_ih"].reshape(3, D), *f["b_hh"].reshape(3, D)], axis=1)
    vec = np.concatenate([vec, np.broadcast_to(np.tile(f["b_se"], GG), (128, GG * S)), mask], axis=1)
    rows = lambda b: np.broadcast_to(np.tile(b, GG), (128, W))
    arrays = {
        "x_in": p["x"].transpose(1, 0, 2).reshape(N, B * D),
        "adj_in": p["adj"].transpose(2, 0, 1).reshape(N, B * N),
        "vec_in": vec,
        "early_in": np.concatenate([f["conv1_w"][:, :, 0].T, f["w_msg"].T, f["w_se"].T], axis=1),
        "conv_in": np.concatenate([f["conv2_w"][:, :, 0::2], f["conv2_w"][:, :, 1::2]], axis=2)
        .transpose(1, 2, 0).reshape(D, TAPS * D),
        "gate_in": np.concatenate([f["w_ih"][:, 0:D].T, f["w_ih"][:, D:2 * D].T, f["w_hh"].T], axis=1),
        "late_in": np.concatenate([p["L1_gnn_weight"], rows(f["b_msg"]), rows(p["L1_gnn_bias"])], axis=1),
    }
    arrays = {k: np.ascontiguousarray(a) for k, a in arrays.items()}
    nc = bacc.Bacc("TRN2", target_bir_lowering=False, num_devices=1)
    args = [nc.dram_tensor(k, a.shape, F32, kind="ExternalInput").ap() for k, a in arrays.items()]
    out = nc.dram_tensor("out", (N, B * D), F32, kind="ExternalOutput").ap()
    gnn_kernel(nc, *args, out)
    r = run_bass_kernel_spmd(nc, [arrays], core_ids=[0])
    return r.results[0]["out"].reshape(N, B, D).transpose(1, 0, 2)
```
